# Optimizing a Trainium2 kernel written in Bass

```python
import numpy as np
import jax
import jax.numpy as jnp

def _softmax(x, axis=-1):
    return jax.nn.softmax(x, axis=axis)

def _gelu(x):
    return jax.nn.gelu(x, approximate=True)

def _silu(x):
    return jax.nn.silu(x)

def _sigmoid(x):
    return jax.nn.sigmoid(x)

def _layernorm(x, axis=-1, eps=1e-05):
    m = jnp.mean(x, axis=axis, keepdims=True)
    v = jnp.var(x, axis=axis, keepdims=True)
    return (x - m) / jnp.sqrt(v + eps)

def _scatter_add(tgt, idx, src, axis=0):
    return tgt.at[idx].add(src)

def _segment_sum(src, seg, n):
    return jax.ops.segment_sum(src, seg, n)
kernel_name = 'mk_adj_resnorm_d2_adj_r2_7364a3'

def setup_inputs(seed: int=0):
    np.random.seed(seed)
    _w = jnp.asarray

    def _rec_inputs():
        import jax
        import jax.numpy as jnp
        _gk = jax.random.key(seed)
        x = 7.22e-05 + 1 * jax.random.normal(jax.random.fold_in(_gk, 1), (16, 512, 512), jnp.float32)
        _a = jax.random.bernoulli(jax.random.fold_in(_gk, 2), 0.0078125, (16, 512, 512))
        _a = jnp.logical_or(_a, jnp.swapaxes(_a, -1, -2))
        _a = jnp.logical_or(_a, jnp.eye(512, dtype=bool))
        _af = _a.astype(jnp.float32)
        _af = _af * jax.random.uniform(jax.random.fold_in(_gk, 3), (16, 512, 512), jnp.float32, 0.05, 4.42607)
        adj = _af
        return (x, adj)
    x, adj = _rec_inputs()

    def _L0_gnn_setup():
        import jax, jax.numpy as jnp
        import numpy as np
        NUM_HEADS = 16
        key = jax.random.key(seed)
        ks = jax.random.split(key, 7)
        B, N, D = (16, 256, 512)
        return {'x': jax.random.normal(ks[0], (B, N, D), dtype=jnp.float32), 'spatial_encoding': jax.random.normal(ks[1], (B, N, N), dtype=jnp.float32), 'edge_encoding': jax.random.normal(ks[2], (B, N, N), dtype=jnp.float32), 'Wq': jax.random.normal(ks[3], (D, D), dtype=jnp.float32) * D ** (-0.5), 'Wk': jax.random.normal(ks[4], (D, D), dtype=jnp.float32) * D ** (-0.5), 'Wv': jax.random.normal(ks[5], (D, D), dtype=jnp.float32) * D ** (-0.5), 'Wo': jax.random.normal(ks[6], (D, D), dtype=jnp.float32) * D ** (-0.5)}
    _L0_gnn_all = _L0_gnn_setup()
    _L0_gnn_in = {k: v for k, v in _L0_gnn_all.items() if k in ('Wq', 'Wk', 'Wv', 'Wo')}
    del _L0_gnn_all

    def _L1_gnn_setup():
        import jax, jax.numpy as jnp
        import numpy as np
        B, N, H, E = (64, 256, 512, 4)
        BN_EPS = 1e-05
        key = jax.random.key(seed)
        ks = jax.random.split(key, 6)
        x = jax.random.normal(ks[0], (B, N, H), dtype=jnp.float32)
        adj = jax.random.uniform(ks[1], (B, N, N), dtype=jnp.float32)
        stdv = 1.0 / np.sqrt(H)
        expert_w = jax.random.uniform(ks[2], (E, H, H), minval=-stdv, maxval=stdv, dtype=jnp.float32)
        r_std = 1.0 / np.sqrt(H)
        router_w = jax.random.uniform(ks[3], (H, E), minval=-r_std, maxval=r_std, dtype=jnp.float32)
        router_b = jax.random.uniform(ks[4], (E,), minval=-r_std, maxval=r_std, dtype=jnp.float32)
        bn_gamma = jnp.ones((E, H), dtype=jnp.float32)
        bn_beta = jnp.zeros((E, H), dtype=jnp.float32)
        return {'x': x, 'adj': adj, 'router_w': router_w, 'router_b': router_b, 'expert_w': expert_w, 'bn_gamma': bn_gamma, 'bn_beta': bn_beta}
    _L1_gnn_all = _L1_gnn_setup()
    _L1_gnn_in = {k: v for k, v in _L1_gnn_all.items() if k in ('router_w', 'router_b', 'expert_w', 'bn_gamma', 'bn_beta')}
    del _L1_gnn_all
    return {'x': x, 'adj': adj, 'L0_gnn_Wq': _L0_gnn_in['Wq'], 'L0_gnn_Wk': _L0_gnn_in['Wk'], 'L0_gnn_Wv': _L0_gnn_in['Wv'], 'L0_gnn_Wo': _L0_gnn_in['Wo'], 'L1_gnn_router_w': _L1_gnn_in['router_w'], 'L1_gnn_router_b': _L1_gnn_in['router_b'], 'L1_gnn_expert_w': _L1_gnn_in['expert_w'], 'L1_gnn_bn_gamma': _L1_gnn_in['bn_gamma'], 'L1_gnn_bn_beta': _L1_gnn_in['bn_beta']}

def reference(x, adj, L0_gnn_Wq, L0_gnn_Wk, L0_gnn_Wv, L0_gnn_Wo, L1_gnn_router_w, L1_gnn_router_b, L1_gnn_expert_w, L1_gnn_bn_gamma, L1_gnn_bn_beta):
    import jax
    import jax.numpy as jnp

    def _L0_gnn_ref(x, spatial_encoding, edge_encoding, Wq, Wk, Wv, Wo):
        import jax, jax.numpy as jnp
        import numpy as np
        NUM_HEADS = 16
        B, N, D = x.shape
        H = NUM_HEADS
        hd = D // H
        scale = D ** (-0.5)

        def split_heads(t):
            return t.reshape(B, N, H, hd).transpose(0, 2, 1, 3)
        q = split_heads(x @ Wq.T)
        k = split_heads(x @ Wk.T)
        v = split_heads(x @ Wv.T)
        bias = (spatial_encoding + edge_encoding)[:, None]
        a = jnp.einsum('bhnd,bhmd->bhnm', q, k) * scale + bias
        row_nonzero = jnp.any(a != 0, axis=-1, keepdims=True)
        a = jnp.where(row_nonzero, a, -jnp.inf)
        p = jax.nn.softmax(a, axis=-1)
        p = jnp.where(jnp.isnan(p), 0.0, p)
        o = jnp.einsum('bhnm,bhmd->bhnd', p, v)
        o = o.transpose(0, 2, 1, 3).reshape(B, N, D)
        return o @ Wo.T

    def _L1_gnn_ref(x, adj, router_w, router_b, expert_w, bn_gamma, bn_beta):
        import jax, jax.numpy as jnp
        import numpy as np
        B, N, H, E = (64, 256, 512, 4)
        BN_EPS = 1e-05
        scores = x.mean(axis=1) @ router_w + router_b
        top1 = jnp.argmax(scores, axis=-1)
        n_exp = expert_w.shape[0]
        W = expert_w[top1]
        support = jnp.einsum('bnh,bhk->bnk', x, W)
        out = jnp.einsum('bnm,bmk->bnk', adj, support)
        s = jax.ops.segment_sum(out.sum(axis=1), top1, num_segments=n_exp)
        ss = jax.ops.segment_sum((out * out).sum(axis=1), top1, num_segments=n_exp)
        cnt = jax.ops.segment_sum(jnp.ones_like(top1, dtype=out.dtype), top1, num_segments=n_exp) * out.shape[1]
        cnt = jnp.maximum(cnt, 1.0)[:, None]
        mean = s / cnt
        var = ss / cnt - mean * mean
        m = mean[top1][:, None, :]
        inv = jax.lax.rsqrt(var[top1][:, None, :] + BN_EPS)
        y = (out - m) * inv * bn_gamma[top1][:, None, :] + bn_beta[top1][:, None, :]
        return jax.nn.relu(y)
    x = _layernorm(x + _L0_gnn_ref(x, adj, adj, L0_gnn_Wq, L0_gnn_Wk, L0_gnn_Wv, L0_gnn_Wo), axis=-1)
    x = _layernorm(x + _L1_gnn_ref(x, adj, L1_gnn_router_w, L1_gnn_router_b, L1_gnn_expert_w, L1_gnn_bn_gamma, L1_gnn_bn_beta), axis=-1)
    return x

_drawn_inputs = setup_inputs


def setup_inputs(seed=0):
    import zlib

    import numpy as np

    out = dict(_drawn_inputs(seed))
    spreads = {'L1_gnn_bn_gamma': (1.0, 0.2), 'L1_gnn_bn_beta': (0.0, 0.1)}
    factors = {}
    for name, (base, spread) in spreads.items():
        noise = np.random.default_rng([zlib.crc32(name.encode()), seed]).standard_normal(out[name].shape)
        drawn = base * np.exp(spread * noise) if base else spread * noise
        out[name] = jnp.asarray(drawn.astype(out[name].dtype))
    for name, factor in factors.items():
        out[name] = (out[name] * factor).astype(out[name].dtype)
    return out
```

```python
from contextlib import ExitStack

import concourse.bass as bass
from concourse import mybir

P = 128
F32 = mybir.dt.float32
F32R = mybir.dt.float32r
I32 = mybir.dt.int32
ALU = mybir.AluOpType
ACT = mybir.ActivationFunctionType
AX = mybir.AxisListType

EPS = 1e-5
HEADS = 16
HG = 4
LEAD = 8
EXP_LEAD = 6

TASKS = {
    0: [("Q", 1), ("V", 0), ("V", 1), ("O-", 0)],
    1: [("K", 1), ("V", 2), ("V", 3), ("O-", 1)],
    2: [("O-", 2)],
    3: [("O-", 3)],
    4: [("Q", 2)],
    5: [("K", 2), ("sum-", 0)],
    6: [("route-", 0)],
    7: [("X-", 0)],
    8: [("Q", 3), ("S-", 0), ("X-", 1)],
    9: [("K", 3), ("S-", 1), ("X-", 2)],
    10: [("S-", 2), ("X-", 3)],
    11: [("S-", 3)],
    12: [("Q+", 0), ("M-", 0)],
    13: [("M-", 1), ("K+", 0)],
    14: [("M-", 2)],
    15: [("M-", 3)],
}
SPLIT_SLOTS = {1: 0, 3: 1, 5: 2, 7: 3, 9: 4}


def build_gnn_layers(nc, x, xT, adj, adjT, wqT, wkT, wvT, woT, router_w, router_b, experts, gammaT, betaT, out):
    B, N, D = x.shape
    NT = N // P
    DT = D // P
    E = experts.shape[0]
    HD = D // HEADS
    GROUPS = HEADS // HG
    UNITS = GROUPS * NT
    STEPS = UNITS * HG
    PAIRS = UNITS // 2
    HALF_SCALE = 0.5 * float(D) ** -0.5
    assert (N, D, E, HD, HG * HD) == (512, 512, 4, 32, P)

    def by_tile(w):
        return w.rearrange("(t p) n -> p t n", p=P)

    ctx = ExitStack()
    with ctx:
        def sb(name, shape, dt=F32):
            return ctx.enter_context(nc.sbuf_tensor(name, shape, dt))

        def pb(name):
            return ctx.enter_context(nc.psum_tensor(name, [P, 512], F32))

        def sem(name):
            return ctx.enter_context(nc.semaphore(name))

        qk_dram = nc.dram_tensor("qk_split", (2, GROUPS, P, 2, DT, P), F32, kind="Internal").ap()
        vo_dram = nc.dram_tensor("vo_split", (2, P, 2, DT, D), F32, kind="Internal").ap()
        ex_dram = nc.dram_tensor("expert_split", (E, P, 2, DT, D), F32, kind="Internal").ap()
        x1_dram = nc.dram_tensor("x1_kept", (B, NT, P, D), F32, kind="Internal").ap()
        mixed_dram = nc.dram_tensor("mixed_kept", (B, DT, P, N), F32, kind="Internal").ap()

        qk_w = sb("qk_w", [P, 2, 2, DT, P], F32R)
        slot_a = sb("slot_a", [P, 2, DT, D], F32R)
        slot_b = sb("slot_b", [P, 2, DT, D], F32R)
        qk_t = sb("qk_t", [P, 2, 2, N], F32R)
        q_stack = sb("q_stack", [P, HG, N], F32R)
        k_stack = sb("k_stack", [P, HG, N], F32R)
        v = sb("v", [P, NT, D])
        xt = sb("xt", [P, 2, DT, N], F32R)
        stage = sb("stage", [P, 4, 512])
        adj_t = sb("adj_t", [P, NT, N])
        x_tile = sb("x_tile", [P, D])
        x1 = sb("x1", [P, NT, D])
        ot = sb("ot", [P, 2, GROUPS, N], F32R)
        att = sb("att", [P, 4, HG, N])
        pt = sb("pt", [P, HG, NT, 2 * P])
        x1t = sb("x1t", [P, 2, DT, P], F32R)
        sup = sb("sup", [P, 2, NT, D], F32R)
        mixed = sb("mixed", [P, N])
        fold1 = sb("fold1", [P, 256])
        fold2 = sb("fold2", [P, 2, HG, P])
        gam = fold1[:, 0:DT * E].rearrange("p (t e) -> p t e", t=DT)
        bet = fold1[:, DT * E:2 * DT * E].rearrange("p (t e) -> p t e", t=DT)
        bn_raw = sb("bn_raw", [P, B, DT, 6])
        ident = sb("ident", [P, P])
        small = sb("small", [P, 64])
        ones, eps_c = small[:, 0:1], small[:, 1:2]
        rb, iota4 = small[:, 4:8], small[:, 8:12]
        total, live, rinv = small[:, 12:16], small[:, 16:20], small[:, 20:24]
        ln_std, ln_rstd = small[:, 24:28], small[:, 28:32]
        xmean = small[:, 32:36]
        rt = small[:, 40:56].rearrange("p (a e) -> p a e", a=4)
        ln_mv = small[:, 56:64].rearrange("p (t s) -> p t s", s=2)
        rw = sb("rw", [P, DT, E])
        nmax = sb("nmax", [P, 4, HG])
        rsum = sb("rsum", [P, 4, HG])
        ln_raw = sb("ln_raw", [P, NT, 6])
        chosen = sb("chosen", [P, B, E])
        pick = sb("pick", [P, 1], I32)

        s_bank = [pb("s_bank0"), pb("s_bank1")]
        t_bank = [pb("t_bank0"), pb("t_bank1")]
        p_bank = [pb("p_bank0"), pb("p_bank1")]
        o_bank = [pb("o_bank0"), pb("o_bank1")]

        pe = {k: sem("pe_" + k) for k in ("score", "turn", "pv", "Q", "K", "V", "O", "sum", "route", "X", "S", "M")}
        act_pt = sem("act_pt"); act_exp = sem("act_exp"); act_ot = sem("act_ot")
        act_hi = {k: sem("act_hi_" + k) for k in "QKXS"}
        act_v = sem("act_v"); act_mixed = sem("act_mixed"); act_std = sem("act_std")
        act_xt = sem("act_xt"); act_at = sem("act_at")
        dve_logit = sem("dve_logit"); dve_stat = sem("dve_stat"); dve_norm = sem("dve_norm")
        dve_lo = {k: sem("dve_lo_" + k) for k in "QKXS"}
        dve_ot = sem("dve_ot"); dve_y = sem("dve_y"); dve_ln = sem("dve_ln"); dve_pick = sem("dve_pick")
        dve_choice = sem("dve_choice"); dve_applied = sem("dve_applied"); dve_chain = sem("dve_chain")
        dve_x1 = sem("dve_x1"); dve_mean = sem("dve_mean"); dve_route = sem("dve_route")
        dve_bn = sem("dve_bn"); dve_xt = sem("dve_xt"); dve_split = sem("dve_split")
        pool_fold1 = sem("pool_fold1"); pool_fold2 = sem("pool_fold2"); pool_at = sem("pool_at")
        pool_const = sem("pool_const")
        ld_const = sem("ld_const"); ld_raw = sem("ld_raw"); st_split = sem("st_split")
        ld_qw = sem("ld_qw"); ld_kw = sem("ld_kw"); ld_wv = sem("ld_wv"); ld_wo = sem("ld_wo"); ld_ex = sem("ld_ex")
        ld_xt = sem("ld_xt"); ld_at = sem("ld_at"); ld_x = sem("ld_x")
        ld_adj = [sem(f"ld_adj{t}") for t in range(NT)]
        q_stacked = sem("q_stacked"); k_stacked = sem("k_stacked")
        st_x1 = sem("st_x1"); st_mixed = sem("st_mixed")
        dve_bnorm = sem("dve_bnorm"); act_bnorm = sem("act_bnorm")
        f_loadx = [sem(f"f_loadx{i}") for i in range(4)]
        f_loadm = [sem(f"f_loadm{i}") for i in range(4)]
        f_store = [sem(f"f_store{i}") for i in range(4)]
        act_relu = sem("act_relu"); pe_back = sem("pe_back"); dve_res = sem("dve_res")
        dve_fln = sem("dve_fln"); act_fstd = sem("act_fstd"); dve_frstd = sem("dve_frstd"); dve_out = sem("dve_out")

        passed_sp = sem("passed_sp"); passed_dve = sem("passed_dve")

        def wait(eng, s, b, per, more):
            if isinstance(b, int):
                if per * b + more > 0:
                    eng.wait_ge(s, per * b + more)
            else:
                assert per * 2 + more > 0
                eng.wait_ge(s, b * per + more)
                if eng.engine == mybir.EngineType.SP:
                    settle(eng)

        def settle(eng):
            eng.sem_inc(passed_sp if eng.engine == mybir.EngineType.SP else passed_dve, 1)

        def dram(ap, b, off):
            if isinstance(b, int):
                return ap[b + off]
            rest = " ".join(f"d{i}" for i in range(2, len(ap.shape)))
            return ap[bass.ds(b + off, 1)].rearrange(f"a d1 {rest} -> (a d1) {rest}")

        def present(name, has_prev, has_next, attends):
            if name.endswith("-"):
                return has_prev
            if name.endswith("+"):
                return has_next
            return attends

        def slot_tasks(u, kind):
            return [t for t in TASKS.get(u, []) if present(t[0], *kind)]

        bank_of = {}
        for k, t in enumerate(t for u in range(UNITS) for t in TASKS[u]):
            bank_of[t] = k % 2
        assert sum(map(len, TASKS.values())) % 2 == 0

        def done_by(b, task):
            name, i = task
            k = name[0] if name[0] in "QKVOXSM" else name
            return {
                "Q": (dve_lo["Q"], GROUPS, (i if name == "Q" else GROUPS) + 1),
                "K": (dve_lo["K"], GROUPS, (i if name == "K" else GROUPS) + 1),
                "V": (act_v, NT, i + 1),
                "O": (dve_y, NT, i + 1 - NT),
                "sum-": (dve_mean, 1, 0),
                "route-": (dve_route, 4, 1 - 4),
                "X": (dve_lo["X"], NT, i + 1 - NT),
                "S": (dve_lo["S"], NT, i + 1 - NT),
                "M": (act_mixed, DT, i + 1 - DT),
            }[k]

        order = [t for u in range(UNITS) for t in TASKS[u]]

        def bank_user_before(task, kind, kind_before):
            at = order.index(task)
            for t in reversed(order[:at]):
                if bank_of[t] == bank_of[task] and present(t[0], *kind):
                    return t, 0
            if kind_before is not None:
                for t in reversed(order):
                    if bank_of[t] == bank_of[task] and present(t[0], *kind_before):
                        return t, 1
            return (("Q+", 0), ("K+", 0))[bank_of[task] != bank_of[("Q+", 0)]], 1

        def wait_bank(eng, b, task, kind, kind_before):
            t, back = bank_user_before(task, kind, kind_before)
            s, per, more = done_by(b, t)
            wait(eng, s, b, per, more - per * back)

        def plan(u, kind):
            tasks = slot_tasks(u, kind)
            total = 4 * len(tasks)
            steps = []
            for j in range(HG):
                lo, hi = total * j // HG, total * (j + 1) // HG
                steps.append([(tasks[c // 4], c % 4) for c in range(lo, hi)])
            return steps

        def three_pass(eng, bank, lhs, rhs, kt, last):
            eng.matmul(bank, lhs(0), rhs(0), start=(kt == 0), stop=False)
            eng.matmul(bank, lhs(0), rhs(1), start=False, stop=False)
            return eng.matmul(bank, lhs(1), rhs(0), start=False, stop=last)

        def pe_chunk(eng, b, task, c, kind, kind_before):
            name, i = task
            bank = p_bank[bank_of[task]]
            if c == 0:
                wait_bank(eng, b, task, kind, kind_before)
            if name[0] in "QK":
                which = "QK".index(name[0])
                g = i if not name.endswith("+") else GROUPS
                if c == 0:
                    wait(eng, (ld_qw, ld_kw)[which], b, GROUPS * 16, (g + 1) * 16)
                    if i == 0:
                        wait(eng, dve_xt, b, 1, 2)
                        wait(eng, act_xt, b, 1, 2)
                mm = three_pass(eng, bank[:, :], lambda h: qk_w[:, which, h, c, :], lambda h: xt[:, h, c, :],
                                c, c == DT - 1)
            elif name == "V":
                if c == 0 and i == 0:
                    wait(eng, ld_wv, b, 16, 16)
                mm = three_pass(eng, bank[:, :], lambda h: xt[:, h, c, i * P:(i + 1) * P],
                                lambda h: slot_a[:, h, c, :], c, c == DT - 1)
            elif name == "O-":
                if c == 0 and i == 0:
                    wait(eng, ld_wo, b, 16, 0)
                    wait(eng, dve_ot, b, PAIRS, 0)
                mm = three_pass(eng, bank[:, :], lambda h: ot[:, h, c, i * P:(i + 1) * P],
                                lambda h: slot_b[:, h, c, :], c, c == DT - 1)
            elif name == "sum-":
                if c == 0:
                    wait(eng, dve_x1, b, NT, 0)
                for t in range(NT):
                    mm = eng.matmul(bank[:, c:c + 1], x1[:, t, c * P:(c + 1) * P], ones[:, :],
                                    start=(t == 0), stop=(t == NT - 1))
            elif name == "route-":
                if c == 0:
                    wait(eng, dve_mean, b, 1, 0)
                mm = eng.matmul(bank[:, 0:E], xmean[:, c:c + 1].to_broadcast([P, P]), rw[:, c, :],
                                start=(c == 0), stop=(c == DT - 1))
            elif name == "X-":
                mm = eng.transpose(bank[:, c * P:(c + 1) * P], x1[:, i, c * P:(c + 1) * P], ident[:, :])
            elif name == "S-":
                if c == 0:
                    wait(eng, dve_lo["X"], b, NT, i + 1 - NT)
                    if i == 0:
                        wait(eng, ld_ex, b, 16, 0)
                mm = three_pass(eng, bank[:, :], lambda h: x1t[:, h, c, :], lambda h: slot_a[:, h, c, :],
                                c, c == DT - 1)
            else:
                if c == 0 and i == 0:
                    wait(eng, dve_lo["S"], b, NT, 0)
                    wait(eng, pool_at, b, NT, 0)
                mm = three_pass(eng, bank[:, :], lambda h: sup[:, h, c, i * P:(i + 1) * P],
                                lambda h: slot_b[:, h, c, :], c, c == NT - 1)
            if c == 3:
                mm.then_inc(pe[name.rstrip("+-")], 1)

        def pe_scores(eng, b, r):
            u, j = divmod(r, HG)
            g, t = divmod(u, NT)
            if j == 0 and t == 0:
                wait(eng, q_stacked, b, GROUPS * 256, (g + 1) * 256)
                wait(eng, k_stacked, b, GROUPS * 256, (g + 1) * 256)
            wait(eng, dve_logit, b, STEPS, r - 1)
            eng.matmul(s_bank[r % 2][:, :], q_stack[:, j, t * P:(t + 1) * P], k_stack[:, j, :],
                       start=True, stop=True).then_inc(pe["score"], 1)

        def pe_turn(eng, b, r):
            u, j = divmod(r, HG)
            wait(eng, dve_norm, b, STEPS, r + 1)
            wait(eng, act_pt, b, STEPS, r - 1)
            for m in range(NT):
                mm = eng.transpose(t_bank[r % 2][:, m * P:(m + 1) * P],
                                   att[:, u % 4, j, m * P:(m + 1) * P], ident[:, :])
            mm.then_inc(pe["turn"], 1)

        def pe_pv(eng, b, u):
            pair, g = u // 2, u // NT
            wait(eng, act_pt, b, STEPS, 4 * u + 4)
            wait(eng, dve_ot, b, PAIRS, pair - 1)
            wait(eng, act_v, b, NT, NT)
            for m in range(NT):
                for j in range(HG):
                    head = g * HG + j
                    mm = eng.matmul(o_bank[pair % 2][j * HD:(j + 1) * HD, 0:2 * P],
                                    v[:, m, head * HD:(head + 1) * HD], pt[:, j, m, :],
                                    start=(m == 0), stop=(m == NT - 1), tile_position=(0, j * HD))
            mm.then_inc(pe["pv"], 1)

        def pe_slot(eng, b, u, kind, kind_before):
            attends, has_next = kind[2], kind[1]
            work = plan(u, kind) if u >= 0 else [[]] * HG
            for j in range(HG):
                r = HG * u + j
                if attends and r >= 0:
                    pe_turn(eng, b, r)
                if (attends and r + LEAD < STEPS) or (has_next and r + LEAD >= STEPS):
                    pe_scores(eng, b, r + LEAD)
                for task, c in work[j]:
                    pe_chunk(eng, b, task, c, kind, kind_before)
            if attends and u >= 0 and u % 2 == 1:
                pe_pv(eng, b, u)

        def act_task(eng, b, task, kind):
            name, i = task
            bank = p_bank[bank_of[task]]
            if name[0] in "QK":
                which = "QK".index(name[0])
                g = i if not name.endswith("+") else GROUPS
                wait(eng, pe[name[0]], b, GROUPS, g + 1)
                wait(eng, (q_stacked, k_stacked)[which], b, GROUPS * 256, g * 256)
                eng.activation(qk_t[:, which, 0, :], bank[:, :], ACT.Copy,
                               scale=HALF_SCALE if which == 0 else 1.0).then_inc(act_hi[name[0]], 1)
            elif name == "V":
                wait(eng, pe["V"], b, NT, i + 1)
                if i == 0:
                    wait(eng, pe["pv"], b, PAIRS, 0)
                eng.activation(v[:, i, :], bank[:, :], ACT.Copy).then_inc(act_v, 1)
            elif name == "X-":
                wait(eng, pe["X"], b, NT, i + 1 - NT)
                wait(eng, pe["S"], b, NT, i - NT)
                eng.activation(x1t[:, 0, :, :].rearrange("p t n -> p (t n)"), bank[:, :],
                               ACT.Copy).then_inc(act_hi["X"], 1)
            elif name == "S-":
                wait(eng, pe["S"], b, NT, i + 1 - NT)
                if i == 0:
                    wait(eng, pe["M"], b, DT, -DT)
                    if isinstance(b, int) and b == 1:
                        eng.wait_ge(st_split, 16 * SPLIT_STORES)
                eng.activation(sup[:, 0, i, :], bank[:, :], ACT.Copy).then_inc(act_hi["S"], 1)
            elif name == "M-":
                wait(eng, pe["M"], b, DT, i + 1 - DT)
                wait(eng, st_mixed, b, 16 * DT, 16 * (i - DT))
                wait(eng, dve_bn, b, DT, i - DT)
                eng.activation(mixed[:, :], bank[:, :], ACT.Copy).then_inc(act_mixed, 1)

        def act_exp_step(eng, b, r):
            u, j = divmod(r, HG)
            wait(eng, dve_logit, b, STEPS, r + 1)
            wait(eng, pool_fold1, b, STEPS, r + 1)
            eng.activation(att[:, u % 4, j, :], att[:, u % 4, j, :], ACT.Exp, bias=nmax[:, u % 4, j:j + 1],
                           scale=-1.0, accum_out=rsum[:, u % 4, j:j + 1]).then_inc(act_exp, 1)

        def act_ot_hi(eng, b, pair):
            g, half = divmod(pair % PAIRS, 2)
            wait(eng, pe["pv"], b, PAIRS, pair + 1)
            if pair == 0:
                wait(eng, pe["O"], b, NT, 2 - NT)
            elif pair == 1:
                wait(eng, pe["O"], b, NT, 0)
            eng.activation(ot[:, 0, g, half * 256:half * 256 + 256], o_bank[pair % 2][:, 0:256],
                           ACT.Copy).then_inc(act_ot, 1)

        def act_slot(eng, b, u, kind, kind_before):
            has_prev, has_next, attends = kind
            work = plan(u, kind) if u >= 0 else [[]] * HG
            if u == 4 and has_prev:
                wait(eng, dve_ln, b, 8, 0)
                eng.activation(ln_std[:, :], ln_mv[:, :, 1], ACT.Sqrt, bias=eps_c[:, :]).then_inc(act_std, 1)
            if u == 4 and has_prev:
                wait(eng, pe["O"], b, NT, 0)
                wait(eng, ld_at, b, 16, 0)
                eng.activation(slot_b[:, 0, :, :], stage[:, :, :], ACT.Copy).then_inc(act_at, 1)
            if u == 10 and has_next:
                wait(eng, pe["K"], b, GROUPS, GROUPS)
                wait(eng, pe["Q"], b, GROUPS, GROUPS)
                wait(eng, ld_xt, b, 16, 32)
                eng.activation(xt[:, 0, :, :], stage[:, :, :], ACT.Copy).then_inc(act_xt, 1)
            if u % 2 == 0 and u >= 0:
                if (u > 0 and attends) or (u == 0 and has_prev):
                    act_ot_hi(eng, b, u // 2 - 1)
            for j in range(HG):
                r = HG * u + j
                if attends and r >= 0:
                    wait(eng, pe["turn"], b, STEPS, r + 1)
                    if u % 2 == 0 and j == 0:
                        wait(eng, pe["pv"], b, PAIRS, u // 2)
                    eng.activation(pt[:, j, :, (u % 2) * P:(u % 2 + 1) * P],
                                   t_bank[r % 2][:, :].rearrange("p (m n) -> p m n", m=NT),
                                   ACT.Copy).then_inc(act_pt, 1)
                e = r + EXP_LEAD
                if e >= 0 and ((attends and e < STEPS) or (has_next and e >= STEPS)):
                    act_exp_step(eng, b, e)
                for task, c in work[j]:
                    if c == 3:
                        act_task(eng, b, task, kind)

        def dve_logits(eng, b, r):
            u, j = divmod(r, HG)
            t = u % NT
            wait(eng, pe["score"], b, STEPS, r + 1)
            if j == 0:
                if u % UNITS < NT:
                    wait(eng, ld_adj[t], b, 16, 16 * (1 + u // UNITS))
                wait(eng, pe["turn"], b, STEPS, 4 * (u - 4) + 4)
            if not isinstance(b, int):
                settle(eng)
            eng.tensor_tensor_reduce(out=att[:, u % 4, j, :], in0=s_bank[r % 2][:, :], in1=adj_t[:, t, :],
                                     scale=-2.0, scalar=3.0e38, op0=ALU.add, op1=ALU.min,
                                     accum_out=nmax[:, u % 4, j:j + 1]).then_inc(dve_logit, 1)

        def dve_stats(eng, b, u):
            wait(eng, pool_fold2, b, STEPS, HG * (u + 1))
            wait(eng, dve_norm, b, STEPS, HG * u)
            eng.tensor_reduce(total[:, :], fold2[:, u % 2, :, :], AX.X, ALU.add).then_inc(dve_stat, 1)
            wait(eng, act_exp, b, STEPS, HG * (u + 1))
            wait(eng, dve_stat, b, 4 * UNITS, 4 * u + 1)
            eng.scalar_tensor_tensor(out=live[:, :], in0=total[:, :], scalar=0.0, in1=nmax[:, u % 4, :],
                                     op0=ALU.not_equal, op1=ALU.logical_or).then_inc(dve_stat, 1)
            eng.reciprocal(rinv[:, :], rsum[:, u % 4, :]).then_inc(dve_stat, 1)
            wait(eng, dve_stat, b, 4 * UNITS, 4 * u + 3)
            eng.tensor_tensor(rinv[:, :], rinv[:, :], live[:, :], ALU.mult).then_inc(dve_stat, 1)
            wait(eng, dve_stat, b, 4 * UNITS, 4 * u + 4)

        def dve_normalise(eng, b, r):
            u, j = divmod(r, HG)
            eng.tensor_scalar(att[:, u % 4, j, :], att[:, u % 4, j, :], rinv[:, j:j + 1], None,
                              ALU.mult).then_inc(dve_norm, 1)

        def dve_low(eng, dst, src, hi, scale=1.0):
            if scale == 1.0:
                return eng.tensor_tensor(dst, src, hi.bitcast(F32), ALU.subtract)
            return eng.scalar_tensor_tensor(out=dst, in0=src, scalar=scale, in1=hi.bitcast(F32), op0=ALU.mult,
                                            op1=ALU.subtract)

        def dve_task(eng, b, task, kind):
            name, i = task
            bank = p_bank[bank_of[task]]
            if name[0] in "QK":
                which = "QK".index(name[0])
                g = i if not name.endswith("+") else GROUPS
                wait(eng, act_hi[name[0]], b, GROUPS, g + 1)
                dve_low(eng, qk_t[:, which, 1, :], bank[:, :], qk_t[:, which, 0, :],
                        HALF_SCALE if which == 0 else 1.0).then_inc(dve_lo[name[0]], 1)
            elif name == "O-":
                wait(eng, pe["O"], b, NT, i + 1 - NT)
                wait(eng, ld_x, b, 16 * NT, 16 * (i + 1 - NT))
                if i == 0:
                    wait(eng, st_x1, b, 16, -16)
                    wait(eng, pe["X"], b, NT, -NT)
                eng.tensor_tensor(x1[:, i, :], bank[:, :], x_tile[:, :], ALU.add).then_inc(dve_y, 1)
                wait(eng, dve_y, b, NT, i + 1 - NT)
                eng.bn_stats(ln_raw[:, i, :], x1[:, i, :]).then_inc(dve_ln, 1)
                wait(eng, dve_ln, b, 8, 2 * i + 1 - 8)
                settle(eng)
                eng.bn_aggr(ln_mv[:, i, :], ln_raw[:, i, :]).then_inc(dve_ln, 1)
            elif name == "sum-":
                wait(eng, pe["sum"], b, 1, 0)
                eng.tensor_scalar(xmean[:, :], bank[:, 0:DT], 1.0 / N, None, ALU.mult).then_inc(dve_mean, 1)
            elif name == "route-":
                wait(eng, pe["route"], b, 1, 0)
                eng.tensor_tensor(rt[:, 0, :], bank[:, 0:E], rb[:, :], ALU.add).then_inc(dve_route, 1)
                wait(eng, dve_route, b, 4, -3)
                eng.tensor_reduce(rt[:, 1, 0:1], rt[:, 0, :], AX.X, ALU.max).then_inc(dve_route, 1)
                wait(eng, dve_route, b, 4, -2)
                eng.tensor_scalar(rt[:, 2, :], rt[:, 0, :], rt[:, 1, 0:1], -float(E), ALU.is_ge,
                                  ALU.mult).then_inc(dve_route, 1)
                wait(eng, dve_route, b, 4, -1)
                eng.tensor_tensor(rt[:, 3, :], rt[:, 2, :], iota4[:, :], ALU.add).then_inc(dve_route, 1)
            elif name in ("X-", "S-"):
                k = name[0]
                wait(eng, act_hi[k], b, NT, i + 1 - NT)
                if k == "X":
                    dve_low(eng, x1t[:, 1, :, :].rearrange("p t n -> p (t n)"), bank[:, :],
                            x1t[:, 0, :, :].rearrange("p t n -> p (t n)")).then_inc(dve_lo["X"], 1)
                else:
                    dve_low(eng, sup[:, 1, i, :], bank[:, :], sup[:, 0, i, :]).then_inc(dve_lo["S"], 1)
            elif name == "M-":
                wait(eng, act_mixed, b, DT, i + 1 - DT)
                row = slice(b - 1, b) if isinstance(b, int) else bass.ds(b - 1, 1)
                eng.bn_stats(bn_raw[:, row, i, :].rearrange("p o s -> p (o s)"), mixed[:, :]).then_inc(dve_bn, 1)

        def dve_choose(eng, b):
            wait(eng, dve_route, b, 4, 0)
            eng.tensor_reduce(rt[:, 1, 1:2], rt[:, 3, :], AX.X, ALU.min).then_inc(dve_pick, 1)
            wait(eng, dve_pick, b, 3, -2)
            eng.tensor_scalar(pick[:, :], rt[:, 1, 1:2], float(E), float(E - 1), ALU.add,
                              ALU.min).then_inc(dve_pick, 1)
            eng.tensor_scalar(rt[:, 2, :], iota4[:, :], float(E), None, ALU.subtract).then_inc(dve_pick, 1)
            wait(eng, dve_pick, b, 3, 0)
            row = slice(b - 1, b) if isinstance(b, int) else bass.ds(b - 1, 1)
            eng.tensor_scalar(chosen[:, row, :], rt[:, 2:3, :], rt[:, 1, 1:2], None,
                              ALU.is_equal).then_inc(dve_choice, 1)

        def dve_slot(eng, b, u, kind, kind_before):
            has_prev, has_next, attends = kind
            work = plan(u, kind) if u >= 0 else [[]] * HG
            if u == 10 and has_next:
                wait(eng, act_xt, b, 1, 2)
                dve_low(eng, xt[:, 1, :, :], stage[:, :, :], xt[:, 0, :, :]).then_inc(dve_xt, 1)
            if u % 2 == 0 and u >= 0 and ((u > 0 and attends) or (u == 0 and has_prev)):
                pair = u // 2 - 1
                g, half = divmod(pair % PAIRS, 2)
                wait(eng, act_ot, b, PAIRS, pair + 1)
                dve_low(eng, ot[:, 1, g, half * 256:half * 256 + 256], o_bank[pair % 2][:, 0:256],
                        ot[:, 0, g, half * 256:half * 256 + 256]).then_inc(dve_ot, 1)
            for j in range(HG):
                r = HG * u + j
                if (attends and r + LEAD < STEPS) or (has_next and r + LEAD >= STEPS):
                    dve_logits(eng, b, r + LEAD)
                nxt_unit = u + 1
                if (attends and nxt_unit < UNITS and nxt_unit >= 0) or (has_next and nxt_unit >= UNITS):
                    if j == 2:
                        dve_stats(eng, b, nxt_unit)
                    if j >= 2:
                        dve_normalise(eng, b, HG * nxt_unit + 2 * (j - 2))
                        dve_normalise(eng, b, HG * nxt_unit + 2 * (j - 2) + 1)
                if u == 4 and j == 0 and has_prev:
                    wait(eng, act_std, b, 1, 0)
                    eng.reciprocal(ln_rstd[:, :], ln_std[:, :]).then_inc(dve_applied, 1)
                    wait(eng, dve_applied, b, 1, 0)
                    for t in range(NT):
                        eng.tensor_scalar(x1[:, t, :], x1[:, t, :], ln_mv[:, t, 0:1], ln_rstd[:, t:t + 1],
                                          ALU.subtract, ALU.mult).then_inc(dve_x1, 1)
                for task, c in work[j]:
                    if c == 3:
                        dve_task(eng, b, task, kind)
                        if task[0] == "route-":
                            dve_choose(eng, b)

        def pool_slot(eng, b, u, kind, kind_before):
            has_prev, has_next, attends = kind
            for j in range(HG):
                r = HG * u + j + LEAD
                if (attends and r < STEPS) or (has_next and r >= STEPS):
                    uu, jj = divmod(r, HG)
                    wait(eng, dve_logit, b, STEPS, r + 1)
                    wait(eng, pool_fold2, b, STEPS, r)
                    a = att[:, uu % 4, jj, :]
                    eng.tensor_tensor(fold1[:, :], a[:, 0:256], a[:, 256:512], ALU.add).then_inc(pool_fold1, 1)
                    wait(eng, pool_fold1, b, STEPS, r + 1)
                    if jj == 0:
                        wait(eng, dve_stat, b, 4 * UNITS, 4 * (uu - 2) + 1)
                    eng.tensor_tensor(fold2[:, uu % 2, jj, :], fold1[:, 0:P], fold1[:, P:2 * P],
                                      ALU.add).then_inc(pool_fold2, 1)
            if has_prev and 4 <= u < 4 + NT:
                t = u - 4
                if t == 0:
                    wait(eng, act_at, b, 1, 0)
                eng.tensor_tensor(slot_b[:, 1, t, :], stage[:, t, :], slot_b[:, 0, t, :].bitcast(F32),
                                  ALU.subtract).then_inc(pool_at, 1)

        def stack(eng, b, which, g):
            src_sem_hi, src_sem_lo = act_hi["QK"[which]], dve_lo["QK"[which]]
            wait(eng, src_sem_hi, b, GROUPS, g + 1)
            wait(eng, src_sem_lo, b, GROUPS, g + 1)
            wait(eng, pe["score"], b, STEPS, NT * HG * g)
            dst = (q_stack, k_stack)[which]
            done = (q_stacked, k_stacked)[which]
            for block in range(4):
                part = block // 2 if which == 0 else block % 2
                for j in range(HG):
                    eng.dma_start(dst[block * HD:(block + 1) * HD, j, :].bitcast(F32),
                                  qk_t[j * HD:(j + 1) * HD, which, part, :].bitcast(F32)).then_inc(done, 16)

        def load_qk_w(eng, b, which, g):
            wait(eng, pe["QK"[which]], b, GROUPS, g)
            eng.dma_start(qk_w[:, which].bitcast(F32), qk_dram[which, g % GROUPS]).then_inc((ld_qw, ld_kw)[which], 16)

        def load_x_tile(eng, b, i):
            wait(eng, dve_y, b, NT, i - NT)
            eng.dma_start(x_tile[:, :], dram(x, b, -1)[i * P:(i + 1) * P, :]).then_inc(ld_x, 16)

        def sp_slot(eng, b, u, kind, kind_before):
            has_prev, has_next, attends = kind
            if u == 0:
                if has_prev:
                    load_x_tile(eng, b, 0)
                    wait(eng, act_xt, b, 1, 1 if attends else 0)
                    wait(eng, dve_xt, b, 1, 1 if attends else 0)
                    eng.dma_start(stage[:, :, :], dram(adjT, b, -1).rearrange("(t p) n -> p t n", p=P))\
                        .then_inc(ld_at, 16)
            if u in (0, 4, 8, 12) and ((u < 12 and attends) or (u == 12 and has_next)):
                g = u // 4 + 1
                if u != 8 or has_next:
                    load_qk_w(eng, b, 0, g + 1)
            if u in (1, 5, 9, 13) and ((u < 13 and attends) or (u == 13 and has_next)):
                g = u // 4 + 1
                if u != 9 or has_next:
                    load_qk_w(eng, b, 1, g + 1)
                stack(eng, b, 0, g)
                stack(eng, b, 1, g)
            if has_prev:
                if u == 1:
                    load_x_tile(eng, b, 1)
                if u == 2:
                    load_x_tile(eng, b, 2)
                    load_x_tile(eng, b, 3)
                if u == 5:
                    wait(eng, dve_x1, b, NT, 0)
                    eng.dma_start(dram(x1_dram, b, -1).rearrange("t p n -> p t n"), x1[:, :, :]).then_inc(st_x1, 16)
                if u == 6:
                    wait(eng, dve_pick, b, 3, -1)
                    if attends:
                        wait(eng, pe["V"], b, NT, NT)
                    else:
                        wait(eng, pe["S"], b, NT, -NT)
                    e = eng.value_load(pick[0:1, 0:1], min_val=0, max_val=E - 1)
                    eng.dma_start(slot_a[:].bitcast(F32),
                                  ex_dram[bass.ds(e, 1)].rearrange("a p h t n -> (a p) h t n")).then_inc(ld_ex, 16)
            if u == 8 and has_next:
                wait(eng, pool_at, b, NT, 0)
                wait(eng, act_at, b, 1, 0)
                wait(eng, act_xt, b, 1, 1)
                wait(eng, dve_xt, b, 1, 1)
                eng.dma_start(stage[:, :, :], dram(xT, b, 1).rearrange("(t p) n -> p t n", p=P)).then_inc(ld_xt, 16)
            if 11 <= u <= 14 and has_next:
                t = u - 11
                wait(eng, dve_logit, b, STEPS, HG * (3 * NT + t + 1))
                eng.dma_start(adj_t[:, t, :], dram(adj, b, 1)[t * P:(t + 1) * P, :]).then_inc(ld_adj[t], 16)
            if u == 12 and has_next:
                wait(eng, pe["S"], b, NT, 0)
                if not has_prev:
                    wait(eng, pe["V"], b, NT, NT)
                eng.dma_start(slot_a[:].bitcast(F32), vo_dram[0]).then_inc(ld_wv, 16)
            if has_prev and u >= 12:
                i = u - 12
                wait(eng, act_mixed, b, DT, i + 1 - DT)
                eng.dma_start(dram(mixed_dram, b, -1)[i], mixed[:, :]).then_inc(st_mixed, 16)
            if u == 15 and attends:
                wait(eng, pe["M"], b, DT, 0)
                if not has_prev:
                    eng.wait_ge(st_split, 16 * SPLIT_STORES)
                eng.dma_start(slot_b[:].bitcast(F32), vo_dram[1]).then_inc(ld_wo, 16)

        raw_buf = [att[:, 0], att[:, 1]]
        hilo_buf = [att[:, 2:4], pt[:, :].rearrange("p a b c -> p (a b c)").rearrange("p (h t n) -> p h t n", h=2, t=4)]
        early = [by_tile(wqT), by_tile(wkT), by_tile(wvT)]
        late = [by_tile(woT)] + [by_tile(experts[e]) for e in range(E)]
        sup_w = sup[:].bitcast(F32)
        SPLIT_STORES = 4 + 4 + 1 + 1 + E

        def dve_split_weights(eng, raw, hilo, n):
            eng.tensor_copy(hilo[:, 0].bitcast(F32R), raw).then_inc(dve_split, 1)
            eng.wait_ge(dve_split, 2 * n + 1)
            eng.tensor_tensor(hilo[:, 1].bitcast(F32R), raw, hilo[:, 0], ALU.subtract).then_inc(dve_split, 1)

        FIRST, MID, LAST, TAIL = (False, True, True), (True, True, True), (True, False, True), (True, False, False)

        def graphs(eng, slot, ahead=None, in_first=None):
            for u in (-2, -1):
                slot(eng, 0, u, FIRST, None)
            for u in range(UNITS):
                slot(eng, 0, u, FIRST, None)
                if in_first:
                    in_first(u)
            for u in range(UNITS):
                slot(eng, 1, u, MID, FIRST)
            with eng.Fori(2, B - 1) as b:
                for u in range(UNITS):
                    slot(eng, b, u, MID, MID)
            for u in range(UNITS):
                slot(eng, B - 1, u, LAST, MID)
            for u in range(UNITS):
                slot(eng, B, u, TAIL, LAST)

        y_buf = [att[:, i] for i in range(4)]
        z_buf = [stage, adj_t, x1, v]
        back_bank = [p_bank[0], p_bank[1], t_bank[0], t_bank[1], s_bank[0], s_bank[1], o_bank[0], o_bank[1]]
        bn_s = fold2[:, 0].rearrange("p a b -> p (a b)")[:, 0:2 * B * DT]\
            .rearrange("p (s b t) -> p s b t", s=2, b=B)
        tmp = fold2[:, 1].rearrange("p a b -> p (a b)")
        bn_tmp = tmp[:, 0:B * DT].rearrange("p (b t) -> p b t", b=B)
        bn_sum = tmp[:, 64:64 + 2 * E * DT].rearrange("p (s e t) -> p s e t", s=2, e=E)
        bn_cnt = tmp[:, 96:96 + E]
        bn_scale = tmp[:, 128:128 + E * DT].rearrange("p (e t) -> p e t", e=E)
        bn_shift = tmp[:, 144:144 + E * DT].rearrange("p (e t) -> p e t", e=E)
        bn_w1 = tmp[:, 160:160 + E * DT].rearrange("p (e t) -> p e t", e=E)
        g_scale = tmp[:, 192:192 + B * DT].rearrange("p (b t) -> p b t", b=B)
        g_shift = tmp[:, 256:256 + B * DT].rearrange("p (b t) -> p b t", b=B)
        bn_tmp2 = tmp[:, 320:320 + B * DT].rearrange("p (b t) -> p b t", b=B)

        block = ctx.enter_context(nc.Block())

        @block.sync
        def _(sp):
            sp.dma_start(raw_buf[0], early[0]).then_inc(ld_raw, 16)
            sp.wait_ge(ld_raw, 16)
            sp.dma_start(raw_buf[1], early[1]).then_inc(ld_raw, 16)
            sp.dma_start(stage[:, :, :], xT[0].rearrange("(t p) n -> p t n", p=P)).then_inc(ld_xt, 16)
            sp.dma_start(rw[:, :, :], router_w.rearrange("(t p) e -> p t e", p=P)).then_inc(ld_const, 16)
            sp.dma_start(rb[:, :], router_b[0:1, :].to_broadcast([P, E])).then_inc(ld_const, 16)
            for which in range(2):
                sp.wait_ge(dve_split, 2 * (which + 1))
                for g in range(GROUPS):
                    sp.dma_start(qk_dram[which, g],
                                 hilo_buf[which][:, :, :, g * P:(g + 1) * P]).then_inc(st_split, 16)
                if which == 0:
                    sp.dma_start(raw_buf[0], early[2]).then_inc(ld_raw, 16)
            sp.wait_ge(dve_split, 6)
            sp.dma_start(vo_dram[0], hilo_buf[0]).then_inc(st_split, 16)
            sp.wait_ge(st_split, 16 * 9)
            load_qk_w(sp, 0, 0, 0)
            load_qk_w(sp, 0, 1, 0)
            sp.dma_start(slot_a[:].bitcast(F32), vo_dram[0]).then_inc(ld_wv, 16)
            for t in range(NT):
                sp.dma_start(adj_t[:, t, :], adj[0, t * P:(t + 1) * P, :]).then_inc(ld_adj[t], 16)
            load_qk_w(sp, 0, 0, 1)
            load_qk_w(sp, 0, 1, 1)
            stack(sp, 0, 0, 0)
            stack(sp, 0, 1, 0)

            def late_weights(u):
                if u in SPLIT_SLOTS:
                    n = SPLIT_SLOTS[u]
                    if n == 0:
                        sp.dma_start(x1[:, :, :], late[0]).then_inc(ld_raw, 16)
                    sp.wait_ge(dve_split, 6 + 2 * (n + 1))
                    sp.dma_start(vo_dram[1] if n == 0 else ex_dram[n - 1], sup_w).then_inc(st_split, 16)
                    if n + 1 < len(late):
                        sp.dma_start(x1[:, :, :], late[n + 1]).then_inc(ld_raw, 16)
            graphs(sp, sp_slot, in_first=late_weights)

            sp.wait_ge(pool_fold2, B * STEPS)
            sp.dma_start(gam[:, :, :], gammaT.rearrange("(t p) e -> p t e", p=P)).then_inc(ld_const, 16)
            sp.dma_start(bet[:, :, :], betaT.rearrange("(t p) e -> p t e", p=P)).then_inc(ld_const, 16)
            sp.wait_ge(st_x1, 16 * B)
            sp.wait_ge(st_mixed, 16 * DT * B)
            sp.wait_ge(act_mixed, DT * B)
            for i in range(4):
                sp.dma_start(y_buf[i], mixed_dram[i].rearrange("t p n -> p t n")).then_inc(f_loadm[i], 16)
            with sp.Fori(0, B // 4 - 1) as k:
                for i in range(4):
                    sp.wait_ge(pe_back, k * (4 * NT) + NT * (i + 1))
                    settle(sp)
                    sp.dma_start(y_buf[i], dram(mixed_dram, k * 4, i + 4).rearrange("t p n -> p t n"))\
                        .then_inc(f_loadm[i], 16)
                    sp.wait_ge(dve_out, k * (4 * NT) + NT * (i + 1))
                    settle(sp)
                    sp.dma_start(dram(out, k * 4, i).rearrange("(t p) n -> p t n", p=P), z_buf[i][:, :, :])\
                        .then_inc(f_store[i], 16)
            for i in range(4):
                sp.wait_ge(dve_out, (B - 4) * NT + NT * (i + 1))
                sp.dma_start(out[B - 4 + i].rearrange("(t p) n -> p t n", p=P), z_buf[i][:, :, :])\
                    .then_inc(f_store[i], 16)
            for i in range(4):
                sp.wait_ge(f_store[i], 16 * (B // 4))

        @block.gpsimd
        def _(pool):
            pool.memset(ident[:, :], 0.0).then_inc(pool_const, 1)
            pool.memset(ones[:, :], 1.0).then_inc(pool_const, 1)
            pool.memset(eps_c[:, :], EPS).then_inc(pool_const, 1)
            for e in range(E):
                pool.memset(iota4[:, e:e + 1], float(e)).then_inc(pool_const, 1)
            pool.wait_ge(pool_const, 3 + E)
            pool.affine_select(out=ident[:, :], in_=ident[:, :], compare_op=ALU.not_equal, fill=1.0, base=0,
                               pattern=[[-1, P]], channel_multiplier=1).then_inc(pool_const, 1)
            graphs(pool, pool_slot)
            pool.wait_ge(st_x1, 16 * B)
            pool.wait_ge(act_mixed, DT * B)
            for i in range(4):
                pool.dma_start(z_buf[i][:, :, :], x1_dram[i].rearrange("t p n -> p t n")).then_inc(f_loadx[i], 16)
            with pool.Fori(0, B // 4 - 1) as k:
                for i in range(4):
                    pool.wait_ge(f_store[i], k * 16 + 16)
                    pool.dma_start(z_buf[i][:, :, :], dram(x1_dram, k * 4, i + 4).rearrange("t p n -> p t n"))\
                        .then_inc(f_loadx[i], 16)

        @block.scalar
        def _(act):
            act.wait_ge(pool_const, 4 + E)
            act.wait_ge(ld_xt, 16)
            act.activation(xt[:, 0, :, :], stage[:, :, :], ACT.Copy).then_inc(act_xt, 1)
            act_task(act, -1, ("Q+", 0), FIRST)
            act_task(act, -1, ("K+", 0), FIRST)
            act.wait_ge(st_split, 16 * 9)
            graphs(act, act_slot)
            act.wait_ge(dve_bnorm, 1)
            act.activation(bn_w1, bn_w1, ACT.Sqrt, bias=eps_c[:, :]).then_inc(act_bnorm, 1)

            def relu(b, i):
                for t in range(DT):
                    at = slice(b + i, b + i + 1) if isinstance(b, int) else bass.ds(b + i, 1)
                    act.activation(y_buf[i % 4][:, t, :], y_buf[i % 4][:, t, :], ACT.Relu,
                                   bias=g_shift[:, at, t], scale=g_scale[:, at, t]).then_inc(act_relu, 1)

            def deviation(count):
                act.wait_ge(dve_fln, count)
                act.activation(ln_std[:, :], ln_mv[:, :, 1], ACT.Sqrt, bias=eps_c[:, :]).then_inc(act_fstd, 1)

            act.wait_ge(dve_bnorm, 2)
            act.wait_ge(f_loadm[0], 16)
            relu(0, 0)
            with act.Fori(0, B // 4 - 1) as k:
                for i in range(4):
                    act.wait_ge(f_loadm[(i + 1) % 4], k * 16 + (16 if i < 3 else 32))
                    relu(k * 4, i + 1)
                    deviation(k * (8 * NT) + 2 * NT * (i + 1))
            for i in range(4):
                if i < 3:
                    act.wait_ge(f_loadm[i + 1], 16 * (B // 4))
                    relu(B - 4, i + 1)
                deviation(2 * NT * (B - 4 + i + 1))

        @block.vector
        def _(dve):
            for n in range(3):
                dve.wait_ge(ld_raw, 16 * (n + 1))
                if n == 2:
                    dve.wait_ge(st_split, 16 * 8)
                dve_split_weights(dve, raw_buf[n % 2], hilo_buf[n % 2], n)
                if n == 0:
                    dve.wait_ge(act_xt, 1)
                    dve_low(dve, xt[:, 1, :, :], stage[:, :, :], xt[:, 0, :, :]).then_inc(dve_xt, 1)
            dve_task(dve, -1, ("Q+", 0), FIRST)
            dve_task(dve, -1, ("K+", 0), FIRST)
            dve.wait_ge(st_split, 16 * 9)
            dve.wait_ge(pool_const, 4 + E)
            dve.wait_ge(ld_const, 32)

            def late_weights(u):
                if u in SPLIT_SLOTS:
                    n = SPLIT_SLOTS[u]
                    dve.wait_ge(ld_raw, 16 * (3 + n + 1))
                    if n:
                        dve.wait_ge(st_split, 16 * (9 + n))
                    dve_split_weights(dve, x1[:, :, :], sup_w, 3 + n)
            graphs(dve, dve_slot, in_first=late_weights)

            chain = [0]

            def link(ins):
                chain[0] += 1
                ins.then_inc(dve_chain, 1)
                dve.wait_ge(dve_chain, chain[0])
            dve.wait_ge(ld_const, 64)
            dve.wait_ge(dve_bn, DT * B)
            dve.wait_ge(dve_choice, B)
            sums, squares = bn_s[:, 0], bn_s[:, 1]
            even, odd = bn_raw[:, :, :, 1], bn_raw[:, :, :, 4]
            half = float(N // 2)
            link(dve.tensor_tensor(sums, even, odd, ALU.add))
            link(dve.tensor_scalar(sums, sums, half, None, ALU.mult))
            link(dve.tensor_tensor(squares, even, even, ALU.mult))
            link(dve.tensor_tensor(bn_tmp, odd, odd, ALU.mult))
            link(dve.tensor_tensor(squares, squares, bn_tmp, ALU.add))
            link(dve.tensor_scalar(squares, squares, half, None, ALU.mult))
            link(dve.tensor_tensor(squares, squares, bn_raw[:, :, :, 2], ALU.add))
            link(dve.tensor_tensor(squares, squares, bn_raw[:, :, :, 5], ALU.add))
            for e in range(E):
                hot = chosen[:, :, e:e + 1].to_broadcast([P, B, DT])
                link(dve.tensor_reduce(bn_cnt[:, e:e + 1], chosen[:, :, e], AX.X, ALU.add))
                for s in range(2):
                    link(dve.tensor_tensor(bn_tmp, bn_s[:, s], hot, ALU.mult))
                    link(dve.tensor_reduce(bn_sum[:, s, e, :], bn_tmp.rearrange("p b t -> p t b"), AX.X, ALU.add))
            link(dve.tensor_scalar(bn_cnt, bn_cnt, float(N), 1.0, ALU.mult, ALU.max))
            link(dve.reciprocal(bn_cnt, bn_cnt))
            for s in range(2):
                link(dve.tensor_tensor(bn_sum[:, s], bn_sum[:, s],
                                       bn_cnt.rearrange("p (e o) -> p e o", o=1).to_broadcast([P, E, DT]), ALU.mult))
            link(dve.tensor_tensor(bn_w1, bn_sum[:, 0], bn_sum[:, 0], ALU.mult))
            dve.tensor_tensor(bn_w1, bn_sum[:, 1], bn_w1, ALU.subtract).then_inc(dve_bnorm, 1)
            dve.wait_ge(act_bnorm, 1)
            link(dve.reciprocal(bn_w1, bn_w1))
            link(dve.tensor_tensor(bn_scale, bn_w1, gam[:, :, :].rearrange("p t e -> p e t"), ALU.mult))
            link(dve.tensor_tensor(bn_w1, bn_sum[:, 0], bn_scale, ALU.mult))
            link(dve.tensor_tensor(bn_shift, bet[:, :, :].rearrange("p t e -> p e t"), bn_w1, ALU.subtract))
            for dst, src in ((g_scale, bn_scale), (g_shift, bn_shift)):
                for e in range(E):
                    hot = chosen[:, :, e:e + 1].to_broadcast([P, B, DT])
                    val = src[:, e:e + 1, :].to_broadcast([P, B, DT])
                    if e == 0:
                        link(dve.tensor_tensor(dst, hot, val, ALU.mult))
                    else:
                        link(dve.tensor_tensor(bn_tmp2, hot, val, ALU.mult))
                        link(dve.tensor_tensor(dst, dst, bn_tmp2, ALU.add))
            dve.tensor_scalar(bn_tmp2, bn_tmp2, 0.0, None, ALU.mult).then_inc(dve_bnorm, 1)
            dve.wait_ge(dve_bnorm, 2)
            dve.tensor_scalar(bn_tmp2, bn_tmp2, 0.0, None, ALU.mult).then_inc(dve_res, 8)

            with dve.Fori(0, B // 4) as k:
                for i in range(4):
                    z = z_buf[i]
                    dve.wait_ge(f_loadx[i], k * 16 + 16)
                    for t in range(NT):
                        dve.wait_ge(pe_back, k * (4 * NT) + NT * i + t + 1)
                        dve.tensor_tensor(z[:, t, :], back_bank[(NT * i + t) % 8][:, :], z[:, t, :],
                                          ALU.add).then_inc(dve_res, 1)
                        dve.wait_ge(dve_res, k * (4 * NT) + 8 + NT * i + t + 1)
                        dve.bn_stats(ln_raw[:, t, :], z[:, t, :]).then_inc(dve_fln, 1)
                        dve.wait_ge(dve_fln, k * (8 * NT) + 2 * (NT * i + t) + 1)
                        settle(dve)
                        dve.bn_aggr(ln_mv[:, t, :], ln_raw[:, t, :]).then_inc(dve_fln, 1)
                    dve.wait_ge(act_fstd, k * 4 + i + 1)
                    dve.reciprocal(ln_rstd[:, :], ln_std[:, :]).then_inc(dve_frstd, 1)
                    dve.wait_ge(dve_frstd, k * 4 + i + 1)
                    for t in range(NT):
                        dve.tensor_scalar(z[:, t, :], z[:, t, :], ln_mv[:, t, 0:1], ln_rstd[:, t:t + 1],
                                          ALU.subtract, ALU.mult).then_inc(dve_out, 1)

        @block.tensor
        def _(eng):
            eng.wait_ge(pool_const, 4 + E)
            eng.wait_ge(ld_const, 32)
            for task in (("Q+", 0), ("K+", 0)):
                for c in range(4):
                    if c == 0:
                        which = "QK".index(task[0][0])
                        eng.wait_ge((ld_qw, ld_kw)[which], 16)
                        eng.wait_ge(act_xt, 1)
                        eng.wait_ge(dve_xt, 1)
                    mm = three_pass(eng, p_bank[bank_of[task]][:, :], lambda h: qk_w[:, which, h, c, :],
                                    lambda h: xt[:, h, c, :], c, c == DT - 1)
                mm.then_inc(pe[task[0][0]], 1)
            graphs(eng, pe_slot)
            with eng.Fori(0, B // 4) as k:
                for i in range(4):
                    eng.wait_ge(act_relu, k * (4 * DT) + DT * (i + 1))
                    for t in range(NT):
                        eng.wait_ge(dve_res, k * (4 * NT) + NT * i + t + 1)
                        for c in range(DT):
                            mm = eng.transpose(back_bank[(NT * i + t) % 8][:, c * P:(c + 1) * P],
                                               y_buf[i][:, c, t * P:(t + 1) * P], ident[:, :])
                        mm.then_inc(pe_back, 1)


_OUT = (16, 512, 512)


def kernel(**inputs):
    import numpy as np
    import concourse.bacc as bacc
    from concourse.bass_utils import run_bass_kernel_spmd

    def flip(a):
        return np.ascontiguousarray(np.swapaxes(np.asarray(a), -1, -2))

    x, adj = inputs["x"], inputs["adj"]
    laid = [
        ("x", np.ascontiguousarray(x)), ("xT", flip(x)), ("adj", np.ascontiguousarray(adj)), ("adjT", flip(adj)),
        ("wqT", flip(inputs["L0_gnn_Wq"])), ("wkT", flip(inputs["L0_gnn_Wk"])),
        ("wvT", flip(inputs["L0_gnn_Wv"])), ("woT", flip(inputs["L0_gnn_Wo"])),
        ("router_w", np.ascontiguousarray(inputs["L1_gnn_router_w"])),
        ("router_b", np.ascontiguousarray(inputs["L1_gnn_router_b"]).reshape(1, -1)),
        ("experts", np.ascontiguousarray(inputs["L1_gnn_expert_w"])),
        ("gammaT", flip(inputs["L1_gnn_bn_gamma"])), ("betaT", flip(inputs["L1_gnn_bn_beta"])),
    ]
    nc = bacc.Bacc("TRN2", target_bir_lowering=False, num_devices=1)
    arrays, args = {}, []
    for name, a in laid:
        arrays[f"in_{name}"] = a
        args.append(nc.dram_tensor(f"in_{name}", a.shape, mybir.dt.from_np(a.dtype), kind="ExternalInput").ap())
    args.append(nc.dram_tensor("out_0", _OUT, F32, kind="ExternalOutput").ap())
    build_gnn_layers(nc, *args)
    r = run_bass_kernel_spmd(nc, [arrays], core_ids=[0])
    return r.results[0]["out_0"]
```

```python
from contextlib import ExitStack

import concourse.bass as bass
from concourse import mybir

P = 128
F32 = mybir.dt.float32
F32R = mybir.dt.float32r
I32 = mybir.dt.int32
ALU = mybir.AluOpType
ACT = mybir.ActivationFunctionType
AX = mybir.AxisListType

EPS = 1e-5
HEADS = 16
HG = 4
LEAD = 8
EXP_LEAD = 6

TASKS = {
    0: [("V", 0), ("V", 1)],
    1: [("V", 2), ("V", 3), ("O-", 0)],
    2: [("Q", 2), ("K", 2), ("O-", 1)],
    3: [("O-", 2), ("O-", 3)],
    4: [("Q", 3)],
    5: [("sum-", 0), ("K", 3)],
    6: [("route-", 0)],
    7: [("X-", 0), ("X-", 1)],
    8: [("S-", 0), ("X-", 2), ("S-", 1)],
    9: [("X-", 3), ("S-", 2)],
    10: [("Q+", 0), ("S-", 3)],
    11: [("M-", 0), ("K+", 0)],
    12: [("M-", 1)],
    13: [("M-", 2)],
    14: [("M-", 3), ("Q+", 1)],
    15: [("K+", 1)],
}
AHEAD = [("Q+", 0), ("K+", 0), ("Q+", 1), ("K+", 1)]
SPLIT_SLOTS = {1: 0, 3: 1, 5: 2, 7: 3, 9: 4}


def build_gnn_layers(nc, x, xT, adj, adjT, wqT, wkT, wvT, woT, router_w, router_b, experts, gammaT, betaT, out):
    B, N, D = x.shape
    NT = N // P
    DT = D // P
    E = experts.shape[0]
    HD = D // HEADS
    GROUPS = HEADS // HG
    UNITS = GROUPS * NT
    STEPS = UNITS * HG
    PAIRS = UNITS // 2
    HALF_SCALE = 0.5 * float(D) ** -0.5
    assert (N, D, E, HD, HG * HD) == (512, 512, 4, 32, P)

    def by_tile(w):
        return w.rearrange("(t p) n -> p t n", p=P)

    ctx = ExitStack()
    with ctx:
        def sb(name, shape, dt=F32):
            return ctx.enter_context(nc.sbuf_tensor(name, shape, dt))

        def pb(name):
            return ctx.enter_context(nc.psum_tensor(name, [P, 512], F32))

        def sem(name):
            return ctx.enter_context(nc.semaphore(name))

        qk_dram = nc.dram_tensor("qk_split", (2, GROUPS, P, 2, DT, P), F32, kind="Internal").ap()
        vo_dram = nc.dram_tensor("vo_split", (2, P, 2, DT, D), F32, kind="Internal").ap()
        ex_dram = nc.dram_tensor("expert_split", (E, P, 2, DT, D), F32, kind="Internal").ap()
        x1_dram = nc.dram_tensor("x1_kept", (B, NT, P, D), F32, kind="Internal").ap()
        mixed_dram = nc.dram_tensor("mixed_kept", (B, DT, P, N), F32, kind="Internal").ap()

        qk_w = sb("qk_w", [P, 2, 2, DT, P], F32R)
        slot_a = sb("slot_a", [P, 2, DT, D], F32R)
        slot_b = sb("slot_b", [P, 2, DT, D], F32R)
        qk_t = sb("qk_t", [P, 2, 2, N], F32R)
        q_stack = sb("q_stack", [P, 2, HG, N], F32R)
        k_stack = sb("k_stack", [P, 2, HG, N], F32R)
        v = sb("v", [P, NT, D])
        xt = sb("xt", [P, 2, DT, N], F32R)
        stage = sb("stage", [P, 4, 512])
        adj_t = sb("adj_t", [P, NT, N])
        x1 = sb("x1", [P, NT, D])
        ot = sb("ot", [P, 2, GROUPS, N], F32R)
        att = sb("att", [P, 4, HG, N])
        pt = sb("pt", [P, HG, NT, 2 * P])
        x1t = sb("x1t", [P, 2, 2, DT, P], F32R)
        sup = sb("sup", [P, 2, NT, D], F32R)
        fold1 = sb("fold1", [P, 256])
        fold2 = sb("fold2", [P, 2, HG, P // 2])
        gam = fold1[:, 0:DT * E].rearrange("p (t e) -> p t e", t=DT)
        bet = fold1[:, DT * E:2 * DT * E].rearrange("p (t e) -> p t e", t=DT)
        bn_raw = sb("bn_raw", [P, B, DT, 6])
        ident = sb("ident", [P, P])
        small = sb("small", [P, 64])
        ones, eps_c = small[:, 0:1], small[:, 1:2]
        rb, iota4 = small[:, 4:8], small[:, 8:12]
        total, live, rinv = small[:, 12:16], small[:, 16:20], small[:, 20:24]
        ln_std, ln_rstd = small[:, 24:28], small[:, 28:32]
        xmean = small[:, 32:36]
        rt = small[:, 40:56].rearrange("p (a e) -> p a e", a=4)
        ln_mv = small[:, 56:64].rearrange("p (t s) -> p t s", s=2)
        rw = sb("rw", [P, DT, E])
        nmax = sb("nmax", [P, 4, HG])
        rsum = sb("rsum", [P, 4, HG])
        ln_raw = sb("ln_raw", [P, NT, 6])
        chosen = sb("chosen", [P, B, E])
        pick = sb("pick", [P, 1], I32)

        s_bank = [pb("s_bank0"), pb("s_bank1")]
        t_bank = [pb("t_bank0"), pb("t_bank1")]
        p_bank = [pb("p_bank0"), pb("p_bank1")]
        o_bank = [pb("o_bank0"), pb("o_bank1")]

        pe = {k: sem("pe_" + k) for k in ("score", "turn", "pv", "Q", "K", "V", "O", "sum", "route", "X", "S", "M")}
        act_pt = sem("act_pt"); act_exp = sem("act_exp"); act_ot = sem("act_ot")
        act_hi = {k: sem("act_hi_" + k) for k in "QKXS"}
        act_v = sem("act_v"); act_mixed = sem("act_mixed"); act_std = sem("act_std")
        act_xt = sem("act_xt"); act_at = sem("act_at")
        dve_logit = sem("dve_logit"); dve_stat = sem("dve_stat"); dve_norm = sem("dve_norm")
        dve_lo = {k: sem("dve_lo_" + k) for k in "QKXS"}
        dve_ot = sem("dve_ot"); dve_y = sem("dve_y"); dve_ln = sem("dve_ln"); dve_pick = sem("dve_pick")
        dve_choice = sem("dve_choice"); dve_applied = sem("dve_applied"); dve_chain = sem("dve_chain")
        dve_x1 = sem("dve_x1"); dve_mean = sem("dve_mean"); dve_route = sem("dve_route")
        dve_bn = sem("dve_bn"); dve_xt = sem("dve_xt"); dve_split = sem("dve_split")
        pool_fold1 = sem("pool_fold1"); pool_halved = sem("pool_halved"); pool_fold2 = sem("pool_fold2"); pool_at = sem("pool_at")
        pool_const = sem("pool_const")
        ld_const = sem("ld_const"); ld_raw = sem("ld_raw"); st_split = sem("st_split")
        ld_qw = sem("ld_qw"); ld_kw = sem("ld_kw"); ld_wv = sem("ld_wv"); ld_wo = sem("ld_wo"); ld_ex = sem("ld_ex")
        ld_xt = sem("ld_xt"); ld_at = sem("ld_at"); ld_x = sem("ld_x")
        ld_adj = [sem(f"ld_adj{t}") for t in range(NT)]
        q_stacked = [sem(f"q_stacked{i}") for i in range(2)]
        k_stacked = [sem(f"k_stacked{i}") for i in range(2)]
        st_x1 = sem("st_x1"); st_mixed = sem("st_mixed")
        dve_bnorm = sem("dve_bnorm"); act_bnorm = sem("act_bnorm")
        f_loadx = [sem(f"f_loadx{i}") for i in range(4)]
        f_loadm = [sem(f"f_loadm{i}") for i in range(4)]
        f_store = [sem(f"f_store{i}") for i in range(4)]
        act_relu = sem("act_relu"); pe_back = sem("pe_back"); dve_res = sem("dve_res")
        dve_fln = sem("dve_fln"); act_fstd = sem("act_fstd"); dve_frstd = sem("dve_frstd"); dve_out = sem("dve_out")

        passed_sp = sem("passed_sp"); passed_dve = sem("passed_dve")

        def wait(eng, s, b, per, more):
            if isinstance(b, int):
                if per * b + more > 0:
                    eng.wait_ge(s, per * b + more)
            else:
                assert per * 2 + more > 0
                eng.wait_ge(s, b * per + more)
                if eng.engine == mybir.EngineType.SP:
                    settle(eng)

        def settle(eng):
            eng.sem_inc(passed_sp if eng.engine == mybir.EngineType.SP else passed_dve, 1)

        def dram(ap, b, off):
            if isinstance(b, int):
                return ap[b + off]
            rest = " ".join(f"d{i}" for i in range(2, len(ap.shape)))
            return ap[bass.ds(b + off, 1)].rearrange(f"a d1 {rest} -> (a d1) {rest}")

        def present(name, has_prev, has_next, attends):
            if name.endswith("-"):
                return has_prev
            if name.endswith("+"):
                return has_next
            return attends

        def slot_tasks(u, kind):
            return [t for t in TASKS.get(u, []) if present(t[0], *kind)]

        EMPTIED = {2 * (pair + 1): pair for pair in range(-1, PAIRS - 1) if pair != 0}
        EMPTIED[3] = 0
        bank_of = {}
        for k, t in enumerate(t for u in range(UNITS) for t in TASKS[u]):
            bank_of[t] = k % 2
        assert sum(map(len, TASKS.values())) % 2 == 0

        def done_by(b, task):
            name, i = task
            k = name[0] if name[0] in "QKVOXSM" else name
            return {
                "Q": (dve_lo["Q"], GROUPS, (i if name == "Q" else GROUPS + i) + 1),
                "K": (dve_lo["K"], GROUPS, (i if name == "K" else GROUPS + i) + 1),
                "V": (act_v, NT, i + 1),
                "O": (dve_y, NT, i + 1 - NT),
                "sum-": (dve_mean, 1, 0),
                "route-": (dve_route, 4, 1 - 4),
                "X": (dve_lo["X"], NT, i + 1 - NT),
                "S": (dve_lo["S"], NT, i + 1 - NT),
                "M": (act_mixed, DT, i + 1 - DT),
            }[k]

        order = [t for u in range(UNITS) for t in TASKS[u]]

        def bank_user_before(task, kind, kind_before):
            at = order.index(task)
            for t in reversed(order[:at]):
                if bank_of[t] == bank_of[task] and present(t[0], *kind):
                    return t, 0
            if kind_before is not None:
                for t in reversed(order):
                    if bank_of[t] == bank_of[task] and present(t[0], *kind_before):
                        return t, 1
            return [t for t in AHEAD if bank_of[t] == bank_of[task]][-1], 1

        def wait_bank(eng, b, task, kind, kind_before):
            t, back = bank_user_before(task, kind, kind_before)
            s, per, more = done_by(b, t)
            wait(eng, s, b, per, more - per * back)

        def plan(u, kind):
            tasks = slot_tasks(u, kind)
            total = 4 * len(tasks)
            steps = []
            for j in range(HG):
                lo, hi = total * j // HG, total * (j + 1) // HG
                steps.append([(tasks[c // 4], c % 4) for c in range(lo, hi)])
            return steps

        def three_pass(eng, bank, lhs, rhs, kt, last):
            eng.matmul(bank, lhs(0), rhs(0), start=(kt == 0), stop=False)
            eng.matmul(bank, lhs(0), rhs(1), start=False, stop=False)
            return eng.matmul(bank, lhs(1), rhs(0), start=False, stop=last)

        def pe_chunk(eng, b, task, c, kind, kind_before):
            name, i = task
            bank = p_bank[bank_of[task]]
            if c == 0:
                wait_bank(eng, b, task, kind, kind_before)
            if name[0] in "QK":
                which = "QK".index(name[0])
                g = i if not name.endswith("+") else GROUPS + i
                if c == 0:
                    wait(eng, (ld_qw, ld_kw)[which], b, GROUPS * 16, (g + 1) * 16)
                    if i == 0:
                        wait(eng, dve_xt, b, 1, 2)
                        wait(eng, act_xt, b, 1, 2)
                mm = three_pass(eng, bank[:, :], lambda h: qk_w[:, which, h, c, :], lambda h: xt[:, h, c, :],
                                c, c == DT - 1)
            elif name == "V":
                if c == 0 and i == 0:
                    wait(eng, ld_wv, b, 16, 16)
                mm = three_pass(eng, bank[:, :], lambda h: xt[:, h, c, i * P:(i + 1) * P],
                                lambda h: slot_a[:, h, c, :], c, c == DT - 1)
            elif name == "O-":
                if c == 0 and i == 0:
                    wait(eng, ld_wo, b, 16, 0)
                    wait(eng, dve_ot, b, PAIRS, 0)
                mm = three_pass(eng, bank[:, :], lambda h: ot[:, h, c, i * P:(i + 1) * P],
                                lambda h: slot_b[:, h, c, :], c, c == DT - 1)
            elif name == "sum-":
                if c == 0:
                    wait(eng, dve_x1, b, NT, 0)
                for t in range(NT):
                    mm = eng.matmul(bank[:, c:c + 1], x1[:, t, c * P:(c + 1) * P], ones[:, :],
                                    start=(t == 0), stop=(t == NT - 1))
            elif name == "route-":
                if c == 0:
                    wait(eng, dve_mean, b, 1, 0)
                mm = eng.matmul(bank[:, 0:E], xmean[:, c:c + 1].to_broadcast([P, P]), rw[:, c, :],
                                start=(c == 0), stop=(c == DT - 1))
            elif name == "X-":
                mm = eng.transpose(bank[:, c * P:(c + 1) * P], x1[:, i, c * P:(c + 1) * P], ident[:, :])
            elif name == "S-":
                if c == 0:
                    wait(eng, dve_lo["X"], b, NT, i + 1 - NT)
                    if i == 0:
                        wait(eng, ld_ex, b, 16, 0)
                mm = three_pass(eng, bank[:, :], lambda h: x1t[:, i % 2, h, c, :], lambda h: slot_a[:, h, c, :],
                                c, c == DT - 1)
            else:
                if c == 0 and i == 0:
                    wait(eng, dve_lo["S"], b, NT, 0)
                    wait(eng, pool_at, b, NT, 0)
                mm = three_pass(eng, bank[:, :], lambda h: sup[:, h, c, i * P:(i + 1) * P],
                                lambda h: slot_b[:, h, c, :], c, c == NT - 1)
            if c == 3:
                mm.then_inc(pe[name.rstrip("+-")], 1)

        def wait_stacked(eng, which, b, g):
            wait(eng, (q_stacked, k_stacked)[which][g % 2], b, GROUPS // 2 * 256, (g // 2 + 1) * 256)

        def pe_scores(eng, b, r):
            u, j = divmod(r, HG)
            g, t = divmod(u, NT)
            if j == 0 and t == 0:
                wait_stacked(eng, 0, b, g)
                wait_stacked(eng, 1, b, g)
            wait(eng, dve_logit, b, STEPS, r - 1)
            eng.matmul(s_bank[r % 2][:, :], q_stack[:, g % 2, j, t * P:(t + 1) * P], k_stack[:, g % 2, j, :],
                       start=True, stop=True).then_inc(pe["score"], 1)

        def pe_turn(eng, b, r):
            u, j = divmod(r, HG)
            wait(eng, dve_norm, b, STEPS, r + 1)
            wait(eng, act_pt, b, STEPS, r - 1)
            for m in range(NT):
                mm = eng.transpose(t_bank[r % 2][:, m * P:(m + 1) * P],
                                   att[:, u % 4, j, m * P:(m + 1) * P], ident[:, :])
            mm.then_inc(pe["turn"], 1)

        def pe_pv(eng, b, u):
            pair, g = u // 2, u // NT
            wait(eng, act_pt, b, STEPS, 4 * u + 4)
            wait(eng, dve_ot, b, PAIRS, pair - 1)
            wait(eng, act_v, b, NT, NT)
            for m in range(NT):
                for j in range(HG):
                    head = g * HG + j
                    mm = eng.matmul(o_bank[pair % 2][j * HD:(j + 1) * HD, 0:2 * P],
                                    v[:, m, head * HD:(head + 1) * HD], pt[:, j, m, :],
                                    start=(m == 0), stop=(m == NT - 1), tile_position=(0, j * HD))
            mm.then_inc(pe["pv"], 1)

        def pe_slot(eng, b, u, kind, kind_before):
            attends, has_next = kind[2], kind[1]
            work = plan(u, kind) if u >= 0 else [[]] * HG
            for j in range(HG):
                r = HG * u + j
                if attends and r >= 0:
                    pe_turn(eng, b, r)
                if (attends and r + LEAD < STEPS) or (has_next and r + LEAD >= STEPS):
                    pe_scores(eng, b, r + LEAD)
                for task, c in work[j]:
                    pe_chunk(eng, b, task, c, kind, kind_before)
            if attends and u >= 0 and u % 2 == 1:
                pe_pv(eng, b, u)

        def act_task(eng, b, task, kind):
            name, i = task
            bank = p_bank[bank_of[task]]
            if name[0] in "QK":
                which = "QK".index(name[0])
                g = i if not name.endswith("+") else GROUPS + i
                wait(eng, pe[name[0]], b, GROUPS, g + 1)
                wait_stacked(eng, which, b, g - 1)
                eng.activation(qk_t[:, which, 0, :], bank[:, :], ACT.Copy,
                               scale=HALF_SCALE if which == 0 else 1.0).then_inc(act_hi[name[0]], 1)
            elif name == "V":
                wait(eng, pe["V"], b, NT, i + 1)
                if i == 0:
                    wait(eng, pe["pv"], b, PAIRS, 0)
                eng.activation(v[:, i, :], bank[:, :], ACT.Copy).then_inc(act_v, 1)
            elif name == "X-":
                wait(eng, pe["X"], b, NT, i + 1 - NT)
                wait(eng, pe["S"], b, NT, i - 1 - NT)
                eng.activation(x1t[:, i % 2, 0, :, :].rearrange("p t n -> p (t n)"), bank[:, :],
                               ACT.Copy).then_inc(act_hi["X"], 1)
            elif name == "S-":
                wait(eng, pe["S"], b, NT, i + 1 - NT)
                if i == 0:
                    wait(eng, pe["M"], b, DT, -DT)
                    if isinstance(b, int) and b == 1:
                        eng.wait_ge(st_split, 16 * SPLIT_STORES)
                eng.activation(sup[:, 0, i, :], bank[:, :], ACT.Copy).then_inc(act_hi["S"], 1)
            elif name == "M-":
                wait(eng, pe["M"], b, DT, i + 1 - DT)
                if i == 0:
                    wait(eng, pe["X"], b, NT, 0)
                    wait(eng, st_x1, b, 16, 0)
                eng.activation(x1[:, i, :], bank[:, :], ACT.Copy).then_inc(act_mixed, 1)

        def act_exp_step(eng, b, r):
            u, j = divmod(r, HG)
            wait(eng, dve_logit, b, STEPS, r + 1)
            wait(eng, pool_fold1, b, STEPS, r + 1)
            eng.activation(att[:, u % 4, j, :], att[:, u % 4, j, :], ACT.Exp, bias=nmax[:, u % 4, j:j + 1],
                           scale=-1.0, accum_out=rsum[:, u % 4, j:j + 1]).then_inc(act_exp, 1)

        def act_ot_hi(eng, b, pair):
            g, half = divmod(pair % PAIRS, 2)
            wait(eng, pe["pv"], b, PAIRS, pair + 1)
            if pair == 0:
                wait(eng, pe["O"], b, NT, 2 - NT)
            elif pair == 1:
                wait(eng, pe["O"], b, NT, 0)
            eng.activation(ot[:, 0, g, half * 256:half * 256 + 256], o_bank[pair % 2][:, 0:256],
                           ACT.Copy).then_inc(act_ot, 1)

        def act_slot(eng, b, u, kind, kind_before):
            has_prev, has_next, attends = kind
            work = plan(u, kind) if u >= 0 else [[]] * HG
            if u == 4 and has_prev:
                wait(eng, dve_ln, b, 8, 0)
                eng.activation(ln_std[:, :], ln_mv[:, :, 1], ACT.Sqrt, bias=eps_c[:, :]).then_inc(act_std, 1)
            if u == 4 and has_prev:
                wait(eng, pe["O"], b, NT, 0)
                wait(eng, ld_at, b, 16, 0)
                eng.activation(slot_b[:, 0, :, :], stage[:, :, :], ACT.Copy).then_inc(act_at, 1)
            if u == 9 and has_next:
                wait(eng, pe["K"], b, GROUPS, GROUPS)
                wait(eng, pe["Q"], b, GROUPS, GROUPS)
                wait(eng, ld_xt, b, 16, 32)
                eng.activation(xt[:, 0, :, :], stage[:, :, :], ACT.Copy).then_inc(act_xt, 1)
            if u in EMPTIED and (attends if u else has_prev):
                act_ot_hi(eng, b, EMPTIED[u])
            for j in range(HG):
                r = HG * u + j
                if attends and r >= 0:
                    wait(eng, pe["turn"], b, STEPS, r + 1)
                    if u % 2 == 0 and j == 0:
                        wait(eng, pe["pv"], b, PAIRS, u // 2)
                    eng.activation(pt[:, j, :, (u % 2) * P:(u % 2 + 1) * P],
                                   t_bank[r % 2][:, :].rearrange("p (m n) -> p m n", m=NT),
                                   ACT.Copy).then_inc(act_pt, 1)
                e = r + EXP_LEAD
                if e >= 0 and ((attends and e < STEPS) or (has_next and e >= STEPS)):
                    act_exp_step(eng, b, e)
                for task, c in work[j]:
                    if c == 3:
                        act_task(eng, b, task, kind)

        def dve_logits(eng, b, r):
            u, j = divmod(r, HG)
            t = u % NT
            wait(eng, pe["score"], b, STEPS, r + 1)
            if j == 0:
                if u % UNITS < NT:
                    wait(eng, ld_adj[t], b, 16, 16 * (1 + u // UNITS))
                wait(eng, pe["turn"], b, STEPS, 4 * (u - 4) + 4)
            if not isinstance(b, int):
                settle(eng)
            eng.tensor_tensor_reduce(out=att[:, u % 4, j, :], in0=s_bank[r % 2][:, :], in1=adj_t[:, t, :],
                                     scale=-2.0, scalar=3.0e38, op0=ALU.add, op1=ALU.min,
                                     accum_out=nmax[:, u % 4, j:j + 1]).then_inc(dve_logit, 1)

        def dve_stats(eng, b, u):
            wait(eng, pool_fold2, b, STEPS, HG * (u + 1))
            wait(eng, dve_norm, b, STEPS, HG * u)
            eng.tensor_reduce(total[:, :], fold2[:, u % 2, :, :], AX.X, ALU.add).then_inc(dve_stat, 1)
            wait(eng, act_exp, b, STEPS, HG * (u + 1))
            wait(eng, dve_stat, b, 4 * UNITS, 4 * u + 1)
            eng.scalar_tensor_tensor(out=live[:, :], in0=total[:, :], scalar=0.0, in1=nmax[:, u % 4, :],
                                     op0=ALU.not_equal, op1=ALU.logical_or).then_inc(dve_stat, 1)
            eng.reciprocal(rinv[:, :], rsum[:, u % 4, :]).then_inc(dve_stat, 1)
            wait(eng, dve_stat, b, 4 * UNITS, 4 * u + 3)
            eng.tensor_tensor(rinv[:, :], rinv[:, :], live[:, :], ALU.mult).then_inc(dve_stat, 1)
            wait(eng, dve_stat, b, 4 * UNITS, 4 * u + 4)

        def dve_normalise(eng, b, r):
            u, j = divmod(r, HG)
            eng.tensor_scalar(att[:, u % 4, j, :], att[:, u % 4, j, :], rinv[:, j:j + 1], None,
                              ALU.mult).then_inc(dve_norm, 1)

        def dve_low(eng, dst, src, hi, scale=1.0):
            if scale == 1.0:
                return eng.tensor_tensor(dst, src, hi.bitcast(F32), ALU.subtract)
            return eng.scalar_tensor_tensor(out=dst, in0=src, scalar=scale, in1=hi.bitcast(F32), op0=ALU.mult,
                                            op1=ALU.subtract)

        def dve_task(eng, b, task, kind):
            name, i = task
            bank = p_bank[bank_of[task]]
            if name[0] in "QK":
                which = "QK".index(name[0])
                g = i if not name.endswith("+") else GROUPS + i
                wait(eng, act_hi[name[0]], b, GROUPS, g + 1)
                dve_low(eng, qk_t[:, which, 1, :], bank[:, :], qk_t[:, which, 0, :],
                        HALF_SCALE if which == 0 else 1.0).then_inc(dve_lo[name[0]], 1)
            elif name == "O-":
                wait(eng, pe["O"], b, NT, i + 1 - NT)
                wait(eng, ld_x, b, 16, 0)
                eng.tensor_tensor(x1[:, i, :], bank[:, :], x1[:, i, :], ALU.add).then_inc(dve_y, 1)
                wait(eng, dve_y, b, NT, i + 1 - NT)
                eng.bn_stats(ln_raw[:, i, :], x1[:, i, :]).then_inc(dve_ln, 1)
                wait(eng, dve_ln, b, 8, 2 * i + 1 - 8)
                settle(eng)
                eng.bn_aggr(ln_mv[:, i, :], ln_raw[:, i, :]).then_inc(dve_ln, 1)
            elif name == "sum-":
                wait(eng, pe["sum"], b, 1, 0)
                eng.tensor_scalar(xmean[:, :], bank[:, 0:DT], 1.0 / N, None, ALU.mult).then_inc(dve_mean, 1)
            elif name == "route-":
                wait(eng, pe["route"], b, 1, 0)
                eng.tensor_tensor(rt[:, 0, :], bank[:, 0:E], rb[:, :], ALU.add).then_inc(dve_route, 1)
                wait(eng, dve_route, b, 4, -3)
                eng.tensor_reduce(rt[:, 1, 0:1], rt[:, 0, :], AX.X, ALU.max).then_inc(dve_route, 1)
                wait(eng, dve_route, b, 4, -2)
                eng.tensor_scalar(rt[:, 2, :], rt[:, 0, :], rt[:, 1, 0:1], -float(E), ALU.is_ge,
                                  ALU.mult).then_inc(dve_route, 1)
                wait(eng, dve_route, b, 4, -1)
                eng.tensor_tensor(rt[:, 3, :], rt[:, 2, :], iota4[:, :], ALU.add).then_inc(dve_route, 1)
            elif name in ("X-", "S-"):
                k = name[0]
                wait(eng, act_hi[k], b, NT, i + 1 - NT)
                if k == "X":
                    dve_low(eng, x1t[:, i % 2, 1, :, :].rearrange("p t n -> p (t n)"), bank[:, :],
                            x1t[:, i % 2, 0, :, :].rearrange("p t n -> p (t n)")).then_inc(dve_lo["X"], 1)
                else:
                    dve_low(eng, sup[:, 1, i, :], bank[:, :], sup[:, 0, i, :]).then_inc(dve_lo["S"], 1)
            elif name == "M-":
                wait(eng, act_mixed, b, DT, i + 1 - DT)
                row = slice(b - 1, b) if isinstance(b, int) else bass.ds(b - 1, 1)
                eng.bn_stats(bn_raw[:, row, i, :].rearrange("p o s -> p (o s)"), x1[:, i, :]).then_inc(dve_bn, 1)

        def dve_choose(eng, b):
            wait(eng, dve_route, b, 4, 0)
            eng.tensor_reduce(rt[:, 1, 1:2], rt[:, 3, :], AX.X, ALU.min).then_inc(dve_pick, 1)
            wait(eng, dve_pick, b, 3, -2)
            eng.tensor_scalar(pick[:, :], rt[:, 1, 1:2], float(E), float(E - 1), ALU.add,
                              ALU.min).then_inc(dve_pick, 1)
            eng.tensor_scalar(rt[:, 2, :], iota4[:, :], float(E), None, ALU.subtract).then_inc(dve_pick, 1)
            wait(eng, dve_pick, b, 3, 0)
            row = slice(b - 1, b) if isinstance(b, int) else bass.ds(b - 1, 1)
            eng.tensor_scalar(chosen[:, row, :], rt[:, 2:3, :], rt[:, 1, 1:2], None,
                              ALU.is_equal).then_inc(dve_choice, 1)

        def dve_slot(eng, b, u, kind, kind_before):
            has_prev, has_next, attends = kind
            work = plan(u, kind) if u >= 0 else [[]] * HG
            if u == 9 and has_next:
                wait(eng, act_xt, b, 1, 2)
                dve_low(eng, xt[:, 1, :, :], stage[:, :, :], xt[:, 0, :, :]).then_inc(dve_xt, 1)
            if u in EMPTIED and (attends if u else has_prev):
                pair = EMPTIED[u]
                g, half = divmod(pair % PAIRS, 2)
                wait(eng, act_ot, b, PAIRS, pair + 1)
                dve_low(eng, ot[:, 1, g, half * 256:half * 256 + 256], o_bank[pair % 2][:, 0:256],
                        ot[:, 0, g, half * 256:half * 256 + 256]).then_inc(dve_ot, 1)
            for j in range(HG):
                r = HG * u + j
                if (attends and r + LEAD < STEPS) or (has_next and r + LEAD >= STEPS):
                    dve_logits(eng, b, r + LEAD)
                nxt_unit = u + 1
                if (attends and nxt_unit < UNITS and nxt_unit >= 0) or (has_next and nxt_unit >= UNITS):
                    if j == 2:
                        dve_stats(eng, b, nxt_unit)
                    if j >= 2:
                        dve_normalise(eng, b, HG * nxt_unit + 2 * (j - 2))
                        dve_normalise(eng, b, HG * nxt_unit + 2 * (j - 2) + 1)
                if u == 4 and j == 0 and has_prev:
                    wait(eng, act_std, b, 1, 0)
                    eng.reciprocal(ln_rstd[:, :], ln_std[:, :]).then_inc(dve_applied, 1)
                    wait(eng, dve_applied, b, 1, 0)
                    for t in range(NT):
                        eng.tensor_scalar(x1[:, t, :], x1[:, t, :], ln_mv[:, t, 0:1], ln_rstd[:, t:t + 1],
                                          ALU.subtract, ALU.mult).then_inc(dve_x1, 1)
                for task, c in work[j]:
                    if c == 3:
                        dve_task(eng, b, task, kind)
                        if task[0] == "route-":
                            dve_choose(eng, b)

        def pool_slot(eng, b, u, kind, kind_before):
            has_prev, has_next, attends = kind
            for j in range(HG):
                r = HG * u + j + LEAD
                if (attends and r < STEPS) or (has_next and r >= STEPS):
                    uu, jj = divmod(r, HG)
                    wait(eng, dve_logit, b, STEPS, r + 1)
                    wait(eng, pool_fold2, b, STEPS, r)
                    a = att[:, uu % 4, jj, :]
                    eng.tensor_tensor(fold1[:, :], a[:, 0:256], a[:, 256:512], ALU.add).then_inc(pool_fold1, 1)
                    wait(eng, pool_fold1, b, STEPS, r + 1)
                    eng.tensor_tensor(fold1[:, 0:P], fold1[:, 0:P], fold1[:, P:2 * P],
                                      ALU.add).then_inc(pool_halved, 1)
                    wait(eng, pool_halved, b, STEPS, r + 1)
                    if jj == 0:
                        wait(eng, dve_stat, b, 4 * UNITS, 4 * (uu - 2) + 1)
                    eng.tensor_tensor(fold2[:, uu % 2, jj, :], fold1[:, 0:P // 2], fold1[:, P // 2:P],
                                      ALU.add).then_inc(pool_fold2, 1)
            if has_prev and 4 <= u < 4 + NT:
                t = u - 4
                if t == 0:
                    wait(eng, act_at, b, 1, 0)
                eng.tensor_tensor(slot_b[:, 1, t, :], stage[:, t, :], slot_b[:, 0, t, :].bitcast(F32),
                                  ALU.subtract).then_inc(pool_at, 1)

        def stack(eng, b, which, g):
            src_sem_hi, src_sem_lo = act_hi["QK"[which]], dve_lo["QK"[which]]
            wait(eng, src_sem_hi, b, GROUPS, g + 1)
            wait(eng, src_sem_lo, b, GROUPS, g + 1)
            wait(eng, pe["score"], b, STEPS, NT * HG * (g - 1))
            dst = (q_stack, k_stack)[which][:, g % 2]
            done = (q_stacked, k_stacked)[which][g % 2]
            for block in range(4):
                part = block // 2 if which == 0 else block % 2
                for j in range(HG):
                    eng.dma_start(dst[block * HD:(block + 1) * HD, j, :].bitcast(F32),
                                  qk_t[j * HD:(j + 1) * HD, which, part, :].bitcast(F32)).then_inc(done, 16)

        def load_qk_w(eng, b, which, g):
            wait(eng, pe["QK"[which]], b, GROUPS, g)
            eng.dma_start(qk_w[:, which].bitcast(F32), qk_dram[which, g % GROUPS]).then_inc((ld_qw, ld_kw)[which], 16)

        def sp_slot(eng, b, u, kind, kind_before):
            has_prev, has_next, attends = kind
            if u == 0:
                if attends:
                    stack(eng, b, 1, 1)
                if has_prev:
                    wait(eng, act_xt, b, 1, 1 if attends else 0)
                    wait(eng, dve_xt, b, 1, 1 if attends else 0)
                    eng.dma_start(stage[:, :, :], dram(adjT, b, -1).rearrange("(t p) n -> p t n", p=P))\
                        .then_inc(ld_at, 16)
            if attends:
                if u == 1:
                    load_qk_w(eng, b, 1, 2)
                if u == 3:
                    stack(eng, b, 0, 2)
                    load_qk_w(eng, b, 0, 3)
                    stack(eng, b, 1, 2)
                    load_qk_w(eng, b, 1, 3)
                if u == 6:
                    stack(eng, b, 0, 3)
                if u == 7:
                    stack(eng, b, 1, 3)
            if has_next:
                if u == 7:
                    load_qk_w(eng, b, 0, 4)
                    load_qk_w(eng, b, 1, 4)
                if u == 10:
                    stack(eng, b, 0, 4)
                    load_qk_w(eng, b, 0, 5)
                if u == 11:
                    stack(eng, b, 1, 4)
                    load_qk_w(eng, b, 1, 5)
                if u == 14:
                    stack(eng, b, 0, 5)
                    load_qk_w(eng, b, 0, 6)
            if has_prev:
                if u == 5:
                    wait(eng, dve_x1, b, NT, 0)
                    eng.dma_start(dram(x1_dram, b, -1).rearrange("t p n -> p t n"), x1[:, :, :]).then_inc(st_x1, 16)
                if u == 6:
                    wait(eng, dve_pick, b, 3, -1)
                    if attends:
                        wait(eng, pe["V"], b, NT, NT)
                    else:
                        wait(eng, pe["S"], b, NT, -NT)
                    e = eng.value_load(pick[0:1, 0:1], min_val=0, max_val=E - 1)
                    eng.dma_start(slot_a[:].bitcast(F32),
                                  ex_dram[bass.ds(e, 1)].rearrange("a p h t n -> (a p) h t n")).then_inc(ld_ex, 16)
            if u == 8 and has_next:
                wait(eng, pool_at, b, NT, 0)
                wait(eng, act_at, b, 1, 0)
                wait(eng, act_xt, b, 1, 1)
                wait(eng, dve_xt, b, 1, 1)
                eng.dma_start(stage[:, :, :], dram(xT, b, 1).rearrange("(t p) n -> p t n", p=P)).then_inc(ld_xt, 16)
            if 11 <= u <= 14 and has_next:
                t = u - 11
                wait(eng, dve_logit, b, STEPS, HG * (3 * NT + t + 1))
                eng.dma_start(adj_t[:, t, :], dram(adj, b, 1)[t * P:(t + 1) * P, :]).then_inc(ld_adj[t], 16)
            if u == 12 and has_next:
                wait(eng, pe["S"], b, NT, 0)
                if not has_prev:
                    wait(eng, pe["V"], b, NT, NT)
                eng.dma_start(slot_a[:].bitcast(F32), vo_dram[0]).then_inc(ld_wv, 16)
            if has_prev and u >= 12:
                i = u - 12
                wait(eng, act_mixed, b, DT, i + 1 - DT)
                eng.dma_start(dram(mixed_dram, b, -1)[i], x1[:, i, :]).then_inc(st_mixed, 16)
            if u == 15 and attends:
                wait(eng, pe["M"], b, DT, 0)
                if not has_prev:
                    eng.wait_ge(st_split, 16 * SPLIT_STORES)
                eng.dma_start(slot_b[:].bitcast(F32), vo_dram[1]).then_inc(ld_wo, 16)
                wait(eng, st_mixed, b, 16 * DT, 0)
                wait(eng, dve_bn, b, DT, 0)
                eng.dma_start(x1[:, :, :], dram(x, b, 0).rearrange("(t p) n -> p t n", p=P)).then_inc(ld_x, 16)

        raw_buf = [att[:, 0], att[:, 1]]
        hilo_buf = [att[:, 2:4], pt[:, :].rearrange("p a b c -> p (a b c)").rearrange("p (h t n) -> p h t n", h=2, t=4)]
        early = [by_tile(wqT), by_tile(wkT), by_tile(wvT)]
        late = [by_tile(woT)] + [by_tile(experts[e]) for e in range(E)]
        sup_w = sup[:].bitcast(F32)
        SPLIT_STORES = 4 + 4 + 1 + 1 + E

        def dve_split_weights(eng, raw, hilo, n):
            eng.tensor_copy(hilo[:, 0].bitcast(F32R), raw).then_inc(dve_split, 1)
            eng.wait_ge(dve_split, 2 * n + 1)
            eng.tensor_tensor(hilo[:, 1].bitcast(F32R), raw, hilo[:, 0], ALU.subtract).then_inc(dve_split, 1)

        FIRST, MID, LAST, TAIL = (False, True, True), (True, True, True), (True, False, True), (True, False, False)

        def graphs(eng, slot, ahead=None, in_first=None):
            for u in (-2, -1):
                slot(eng, 0, u, FIRST, None)
            for u in range(UNITS):
                slot(eng, 0, u, FIRST, None)
                if in_first:
                    in_first(u)
            for u in range(UNITS):
                slot(eng, 1, u, MID, FIRST)
            with eng.Fori(2, B - 1) as b:
                for u in range(UNITS):
                    slot(eng, b, u, MID, MID)
            for u in range(UNITS):
                slot(eng, B - 1, u, LAST, MID)
            for u in range(UNITS):
                slot(eng, B, u, TAIL, LAST)

        y_buf = [att[:, i] for i in range(4)]
        z_buf = [stage, adj_t, x1, v]
        back_bank = [p_bank[0], p_bank[1], t_bank[0], t_bank[1], s_bank[0], s_bank[1], o_bank[0], o_bank[1]]
        bn_all = fold2[:, :].rearrange("p a b c -> p (a b c)")
        bn_s = bn_all[:, 0:2 * B * DT].rearrange("p (s b t) -> p s b t", s=2, b=B)
        tmp = bn_all[:, P:4 * P]
        bn_tmp = tmp[:, 0:B * DT].rearrange("p (b t) -> p b t", b=B)
        bn_sum = tmp[:, 64:64 + 2 * E * DT].rearrange("p (s e t) -> p s e t", s=2, e=E)
        bn_cnt = tmp[:, 96:96 + E]
        bn_scale = tmp[:, 128:128 + E * DT].rearrange("p (e t) -> p e t", e=E)
        bn_shift = tmp[:, 144:144 + E * DT].rearrange("p (e t) -> p e t", e=E)
        bn_w1 = tmp[:, 160:160 + E * DT].rearrange("p (e t) -> p e t", e=E)
        g_scale = tmp[:, 192:192 + B * DT].rearrange("p (b t) -> p b t", b=B)
        g_shift = tmp[:, 256:256 + B * DT].rearrange("p (b t) -> p b t", b=B)
        bn_tmp2 = tmp[:, 320:320 + B * DT].rearrange("p (b t) -> p b t", b=B)

        block = ctx.enter_context(nc.Block())

        @block.sync
        def _(sp):
            sp.dma_start(raw_buf[0], early[0]).then_inc(ld_raw, 16)
            sp.wait_ge(ld_raw, 16)
            sp.dma_start(raw_buf[1], early[1]).then_inc(ld_raw, 16)
            sp.dma_start(stage[:, :, :], xT[0].rearrange("(t p) n -> p t n", p=P)).then_inc(ld_xt, 16)
            sp.dma_start(rw[:, :, :], router_w.rearrange("(t p) e -> p t e", p=P)).then_inc(ld_const, 16)
            sp.dma_start(rb[:, :], router_b[0:1, :].to_broadcast([P, E])).then_inc(ld_const, 16)
            for which in range(2):
                sp.wait_ge(dve_split, 2 * (which + 1))
                for g in range(GROUPS):
                    sp.dma_start(qk_dram[which, g],
                                 hilo_buf[which][:, :, :, g * P:(g + 1) * P]).then_inc(st_split, 16)
                if which == 0:
                    sp.dma_start(raw_buf[0], early[2]).then_inc(ld_raw, 16)
            sp.wait_ge(dve_split, 6)
            sp.dma_start(vo_dram[0], hilo_buf[0]).then_inc(st_split, 16)
            sp.wait_ge(st_split, 16 * 9)
            load_qk_w(sp, 0, 0, 0)
            load_qk_w(sp, 0, 1, 0)
            sp.dma_start(slot_a[:].bitcast(F32), vo_dram[0]).then_inc(ld_wv, 16)
            for t in range(NT):
                sp.dma_start(adj_t[:, t, :], adj[0, t * P:(t + 1) * P, :]).then_inc(ld_adj[t], 16)
            load_qk_w(sp, 0, 0, 1)
            load_qk_w(sp, 0, 1, 1)
            stack(sp, 0, 0, 0)
            stack(sp, 0, 1, 0)
            stack(sp, 0, 0, 1)
            load_qk_w(sp, 0, 0, 2)

            def late_weights(u):
                if u in SPLIT_SLOTS:
                    n = SPLIT_SLOTS[u]
                    if n == 0:
                        sp.dma_start(x1[:, :, :], late[0]).then_inc(ld_raw, 16)
                    sp.wait_ge(dve_split, 6 + 2 * (n + 1))
                    sp.dma_start(vo_dram[1] if n == 0 else ex_dram[n - 1], sup_w).then_inc(st_split, 16)
                    if n + 1 < len(late):
                        sp.dma_start(x1[:, :, :], late[n + 1]).then_inc(ld_raw, 16)
            graphs(sp, sp_slot, in_first=late_weights)

            sp.wait_ge(pool_fold2, B * STEPS)
            sp.dma_start(gam[:, :, :], gammaT.rearrange("(t p) e -> p t e", p=P)).then_inc(ld_const, 16)
            sp.dma_start(bet[:, :, :], betaT.rearrange("(t p) e -> p t e", p=P)).then_inc(ld_const, 16)
            sp.wait_ge(st_x1, 16 * B)
            sp.wait_ge(st_mixed, 16 * DT * B)
            sp.wait_ge(act_mixed, DT * B)
            sp.wait_ge(dve_bn, DT * B)
            for i in range(4):
                sp.dma_start(y_buf[i], mixed_dram[i].rearrange("t p n -> p t n")).then_inc(f_loadm[i], 16)
                sp.dma_start(z_buf[i][:, :, :], x1_dram[i].rearrange("t p n -> p t n")).then_inc(f_loadx[i], 16)

            def mixed_next(k, i):
                wait(sp, pe_back, k, 4 * NT, NT * (i + 1))
                sp.dma_start(y_buf[i], dram(mixed_dram, 4 * k, i + 4).rearrange("t p n -> p t n"))\
                    .then_inc(f_loadm[i], 16)

            def store(k, i):
                wait(sp, dve_out, k, 4 * NT, NT * (i + 1))
                sp.dma_start(dram(out, 4 * k, i).rearrange("(t p) n -> p t n", p=P), z_buf[i][:, :, :])\
                    .then_inc(f_store[i], 16)

            def x1_next(k, i):
                wait(sp, f_store[i], k, 16, 16)
                sp.dma_start(z_buf[i][:, :, :], dram(x1_dram, 4 * k, i + 4).rearrange("t p n -> p t n"))\
                    .then_inc(f_loadx[i], 16)
            rounds = B // 4
            for i in range(4):
                mixed_next(0, i)
                store(0, i)
                if i:
                    x1_next(0, i - 1)
            with sp.Fori(1, rounds - 1) as k:
                for i in range(4):
                    mixed_next(k, i)
                    store(k, i)
                    x1_next(k - 1 if i == 0 else k, (i - 1) % 4)
            x1_next(rounds - 2, 3)
            for i in range(4):
                store(rounds - 1, i)
            for i in range(4):
                sp.wait_ge(f_store[i], 16 * rounds)

        @block.gpsimd
        def _(pool):
            pool.memset(ident[:, :], 0.0).then_inc(pool_const, 1)
            pool.memset(ones[:, :], 1.0).then_inc(pool_const, 1)
            pool.memset(eps_c[:, :], EPS).then_inc(pool_const, 1)
            for e in range(E):
                pool.memset(iota4[:, e:e + 1], float(e)).then_inc(pool_const, 1)
            pool.wait_ge(pool_const, 3 + E)
            pool.affine_select(out=ident[:, :], in_=ident[:, :], compare_op=ALU.not_equal, fill=1.0, base=0,
                               pattern=[[-1, P]], channel_multiplier=1).then_inc(pool_const, 1)
            graphs(pool, pool_slot)

        @block.scalar
        def _(act):
            act.wait_ge(pool_const, 4 + E)
            act.wait_ge(ld_xt, 16)
            act.activation(xt[:, 0, :, :], stage[:, :, :], ACT.Copy).then_inc(act_xt, 1)
            for task in AHEAD:
                act_task(act, -1, task, FIRST)
            act.wait_ge(st_split, 16 * 9)
            graphs(act, act_slot)
            act.wait_ge(dve_bnorm, 1)
            act.activation(bn_w1, bn_w1, ACT.Sqrt, bias=eps_c[:, :]).then_inc(act_bnorm, 1)

            def relu(b, i):
                for t in range(DT):
                    at = slice(b + i, b + i + 1) if isinstance(b, int) else bass.ds(b + i, 1)
                    act.activation(y_buf[i % 4][:, t, :], y_buf[i % 4][:, t, :], ACT.Relu,
                                   bias=g_shift[:, at, t], scale=g_scale[:, at, t]).then_inc(act_relu, 1)

            def deviation(count):
                act.wait_ge(dve_fln, count)
                act.activation(ln_std[:, :], ln_mv[:, :, 1], ACT.Sqrt, bias=eps_c[:, :]).then_inc(act_fstd, 1)

            act.wait_ge(dve_bnorm, 2)
            act.wait_ge(f_loadm[0], 16)
            relu(0, 0)
            with act.Fori(0, B // 4 - 1) as k:
                for i in range(4):
                    act.wait_ge(f_loadm[(i + 1) % 4], k * 16 + (16 if i < 3 else 32))
                    relu(k * 4, i + 1)
                    deviation(k * (8 * NT) + 2 * NT * (i + 1))
            for i in range(4):
                if i < 3:
                    act.wait_ge(f_loadm[i + 1], 16 * (B // 4))
                    relu(B - 4, i + 1)
                deviation(2 * NT * (B - 4 + i + 1))

        @block.vector
        def _(dve):
            for n in range(3):
                dve.wait_ge(ld_raw, 16 * (n + 1))
                if n == 2:
                    dve.wait_ge(st_split, 16 * 8)
                dve_split_weights(dve, raw_buf[n % 2], hilo_buf[n % 2], n)
                if n == 0:
                    dve.wait_ge(act_xt, 1)
                    dve_low(dve, xt[:, 1, :, :], stage[:, :, :], xt[:, 0, :, :]).then_inc(dve_xt, 1)
            for task in AHEAD:
                dve_task(dve, -1, task, FIRST)
            dve.wait_ge(st_split, 16 * 9)
            dve.wait_ge(pool_const, 4 + E)
            dve.wait_ge(ld_const, 32)

            def late_weights(u):
                if u in SPLIT_SLOTS:
                    n = SPLIT_SLOTS[u]
                    dve.wait_ge(ld_raw, 16 * (3 + n + 1))
                    if n:
                        dve.wait_ge(st_split, 16 * (9 + n))
                    dve_split_weights(dve, x1[:, :, :], sup_w, 3 + n)
            graphs(dve, dve_slot, in_first=late_weights)

            chain = [0]

            def link(ins):
                chain[0] += 1
                ins.then_inc(dve_chain, 1)
                dve.wait_ge(dve_chain, chain[0])
            dve.wait_ge(ld_const, 64)
            dve.wait_ge(dve_bn, DT * B)
            dve.wait_ge(dve_choice, B)
            sums, squares = bn_s[:, 0], bn_s[:, 1]
            even, odd = bn_raw[:, :, :, 1], bn_raw[:, :, :, 4]
            half = float(N // 2)
            link(dve.tensor_tensor(sums, even, odd, ALU.add))
            link(dve.tensor_scalar(sums, sums, half, None, ALU.mult))
            link(dve.tensor_tensor(squares, even, even, ALU.mult))
            link(dve.tensor_tensor(bn_tmp, odd, odd, ALU.mult))
            link(dve.tensor_tensor(squares, squares, bn_tmp, ALU.add))
            link(dve.tensor_scalar(squares, squares, half, None, ALU.mult))
            link(dve.tensor_tensor(squares, squares, bn_raw[:, :, :, 2], ALU.add))
            link(dve.tensor_tensor(squares, squares, bn_raw[:, :, :, 5], ALU.add))
            for e in range(E):
                hot = chosen[:, :, e:e + 1].to_broadcast([P, B, DT])
                link(dve.tensor_reduce(bn_cnt[:, e:e + 1], chosen[:, :, e], AX.X, ALU.add))
                for s in range(2):
                    link(dve.tensor_tensor(bn_tmp, bn_s[:, s], hot, ALU.mult))
                    link(dve.tensor_reduce(bn_sum[:, s, e, :], bn_tmp.rearrange("p b t -> p t b"), AX.X, ALU.add))
            link(dve.tensor_scalar(bn_cnt, bn_cnt, float(N), 1.0, ALU.mult, ALU.max))
            link(dve.reciprocal(bn_cnt, bn_cnt))
            for s in range(2):
                link(dve.tensor_tensor(bn_sum[:, s], bn_sum[:, s],
                                       bn_cnt.rearrange("p (e o) -> p e o", o=1).to_broadcast([P, E, DT]), ALU.mult))
            link(dve.tensor_tensor(bn_w1, bn_sum[:, 0], bn_sum[:, 0], ALU.mult))
            dve.tensor_tensor(bn_w1, bn_sum[:, 1], bn_w1, ALU.subtract).then_inc(dve_bnorm, 1)
            dve.wait_ge(act_bnorm, 1)
            link(dve.reciprocal(bn_w1, bn_w1))
            link(dve.tensor_tensor(bn_scale, bn_w1, gam[:, :, :].rearrange("p t e -> p e t"), ALU.mult))
            link(dve.tensor_tensor(bn_w1, bn_sum[:, 0], bn_scale, ALU.mult))
            link(dve.tensor_tensor(bn_shift, bet[:, :, :].rearrange("p t e -> p e t"), bn_w1, ALU.subtract))
            for dst, src in ((g_scale, bn_scale), (g_shift, bn_shift)):
                for e in range(E):
                    hot = chosen[:, :, e:e + 1].to_broadcast([P, B, DT])
                    val = src[:, e:e + 1, :].to_broadcast([P, B, DT])
                    if e == 0:
                        link(dve.tensor_tensor(dst, hot, val, ALU.mult))
                    else:
                        link(dve.tensor_tensor(bn_tmp2, hot, val, ALU.mult))
                        link(dve.tensor_tensor(dst, dst, bn_tmp2, ALU.add))
            dve.tensor_scalar(bn_tmp2, bn_tmp2, 0.0, None, ALU.mult).then_inc(dve_bnorm, 1)
            dve.wait_ge(dve_bnorm, 2)
            dve.tensor_scalar(bn_tmp2, bn_tmp2, 0.0, None, ALU.mult).then_inc(dve_res, 8)

            with dve.Fori(0, B // 4) as k:
                for i in range(4):
                    z = z_buf[i]
                    dve.wait_ge(f_loadx[i], k * 16 + 16)
                    for t in range(NT):
                        dve.wait_ge(pe_back, k * (4 * NT) + NT * i + t + 1)
                        dve.tensor_tensor(z[:, t, :], back_bank[(NT * i + t) % 8][:, :], z[:, t, :],
                                          ALU.add).then_inc(dve_res, 1)
                        dve.wait_ge(dve_res, k * (4 * NT) + 8 + NT * i + t + 1)
                        dve.bn_stats(ln_raw[:, t, :], z[:, t, :]).then_inc(dve_fln, 1)
                        dve.wait_ge(dve_fln, k * (8 * NT) + 2 * (NT * i + t) + 1)
                        settle(dve)
                        dve.bn_aggr(ln_mv[:, t, :], ln_raw[:, t, :]).then_inc(dve_fln, 1)
                    dve.wait_ge(act_fstd, k * 4 + i + 1)
                    dve.reciprocal(ln_rstd[:, :], ln_std[:, :]).then_inc(dve_frstd, 1)
                    dve.wait_ge(dve_frstd, k * 4 + i + 1)
                    for t in range(NT):
                        dve.tensor_scalar(z[:, t, :], z[:, t, :], ln_mv[:, t, 0:1], ln_rstd[:, t:t + 1],
                                          ALU.subtract, ALU.mult).then_inc(dve_out, 1)

        @block.tensor
        def _(eng):
            eng.wait_ge(pool_const, 4 + E)
            eng.wait_ge(ld_const, 32)
            for n, task in enumerate(AHEAD):
                earlier = [t for t in AHEAD[:n] if bank_of[t] == bank_of[task]]
                if earlier:
                    s, per, more = done_by(-1, earlier[-1])
                    wait(eng, s, -1, per, more)
                which = "QK".index(task[0][0])
                eng.wait_ge((ld_qw, ld_kw)[which], 16 * (task[1] + 1))
                eng.wait_ge(act_xt, 1)
                eng.wait_ge(dve_xt, 1)
                for c in range(DT):
                    mm = three_pass(eng, p_bank[bank_of[task]][:, :], lambda h: qk_w[:, which, h, c, :],
                                    lambda h: xt[:, h, c, :], c, c == DT - 1)
                mm.then_inc(pe[task[0][0]], 1)
            graphs(eng, pe_slot)
            with eng.Fori(0, B // 4) as k:
                for i in range(4):
                    eng.wait_ge(act_relu, k * (4 * DT) + DT * (i + 1))
                    for t in range(NT):
                        eng.wait_ge(dve_res, k * (4 * NT) + NT * i + t + 1)
                        for c in range(DT):
                            mm = eng.transpose(back_bank[(NT * i + t) % 8][:, c * P:(c + 1) * P],
                                               y_buf[i][:, c, t * P:(t + 1) * P], ident[:, :])
                        mm.then_inc(pe_back, 1)


_OUT = (16, 512, 512)


def kernel(**inputs):
    import numpy as np
    import concourse.bacc as bacc
    from concourse.bass_utils import run_bass_kernel_spmd

    def flip(a):
        return np.ascontiguousarray(np.swapaxes(np.asarray(a), -1, -2))

    x, adj = inputs["x"], inputs["adj"]
    laid = [
        ("x", np.ascontiguousarray(x)), ("xT", flip(x)), ("adj", np.ascontiguousarray(adj)), ("adjT", flip(adj)),
        ("wqT", flip(inputs["L0_gnn_Wq"])), ("wkT", flip(inputs["L0_gnn_Wk"])),
        ("wvT", flip(inputs["L0_gnn_Wv"])), ("woT", flip(inputs["L0_gnn_Wo"])),
        ("router_w", np.ascontiguousarray(inputs["L1_gnn_router_w"])),
        ("router_b", np.ascontiguousarray(inputs["L1_gnn_router_b"]).reshape(1, -1)),
        ("experts", np.ascontiguousarray(inputs["L1_gnn_expert_w"])),
        ("gammaT", flip(inputs["L1_gnn_bn_gamma"])), ("betaT", flip(inputs["L1_gnn_bn_beta"])),
    ]
    nc = bacc.Bacc("TRN2", target_bir_lowering=False, num_devices=1, dynamic_dma_scratch_size=1024)
    arrays, args = {}, []
    for name, a in laid:
        arrays[f"in_{name}"] = a
        args.append(nc.dram_tensor(f"in_{name}", a.shape, mybir.dt.from_np(a.dtype), kind="ExternalInput").ap())
    args.append(nc.dram_tensor("out_0", _OUT, F32, kind="ExternalOutput").ap())
    build_gnn_layers(nc, *args)
    r = run_bass_kernel_spmd(nc, [arrays], core_ids=[0])
    return r.results[0]["out_0"]
```

```python
from contextlib import ExitStack

import concourse.bass as bass
from concourse import mybir

P = 128
F32 = mybir.dt.float32
F32R = mybir.dt.float32r
I32 = mybir.dt.int32
ALU = mybir.AluOpType
ACT = mybir.ActivationFunctionType
AX = mybir.AxisListType

EPS = 1e-5
HEADS = 16
HG = 4
LEAD = 12
EXP_LEAD = 10

NORM_UNITS = 2

TASKS = [
    ("V", 0), ("V", 1), ("V", 2), ("V", 3),
    ("K", 2), ("O-", 0), ("O-", 1), ("Q", 3), ("O-", 2), ("K", 3),
    ("O-", 3),
    ("Q+", 0), ("sum-", 0), ("route-", 0),
    ("X-", 0), ("X-", 1), ("K+", 0),
    ("S-", 0), ("X-", 2), ("S-", 1), ("X-", 3), ("S-", 2), ("S-", 3),
    ("Q+", 1), ("M-", 0), ("K+", 1), ("M-", 1), ("M-", 2), ("Q+", 2), ("M-", 3),
]
COST = {"sum-": 0.4, "route-": 0.1, "X-": 0.2}
HALF_SLOTS = [4, 4] * 2 + [3, 3] * 4 + [4, 0] + [4, 2] + [3, 2.6] + [3.3, 3.3] * 7
AHEAD = [("Q+", 0), ("K+", 0), ("Q+", 1), ("K+", 1), ("Q+", 2)]
SPLIT_SLOTS = {1: 0, 3: 1, 5: 2, 7: 3, 9: 4}


def build_gnn_layers(nc, x, xT, adj, adjT, wqT, wkT, wvT, woT, router_w, router_b, experts, gammaT, betaT, out):
    B, N, D = x.shape
    NT = N // P
    DT = D // P
    E = experts.shape[0]
    HD = D // HEADS
    GROUPS = HEADS // HG
    UNITS = GROUPS * NT
    STEPS = UNITS * HG
    PAIRS = UNITS // 2
    HALF_SCALE = 0.5 * float(D) ** -0.5
    assert (N, D, E, HD, HG * HD) == (512, 512, 4, 32, P)

    def by_tile(w):
        return w.rearrange("(t p) n -> p t n", p=P)

    ctx = ExitStack()
    with ctx:
        def sb(name, shape, dt=F32):
            return ctx.enter_context(nc.sbuf_tensor(name, shape, dt))

        def pb(name):
            return ctx.enter_context(nc.psum_tensor(name, [P, 512], F32))

        def sem(name):
            return ctx.enter_context(nc.semaphore(name))

        qk_dram = nc.dram_tensor("qk_split", (2, GROUPS, P, 2, DT, P), F32, kind="Internal").ap()
        vo_dram = nc.dram_tensor("vo_split", (2, P, 2, DT, D), F32, kind="Internal").ap()
        ex_dram = nc.dram_tensor("expert_split", (E, P, 2, DT, D), F32, kind="Internal").ap()
        x1_dram = nc.dram_tensor("x1_kept", (B, NT, P, D), F32, kind="Internal").ap()
        mixed_dram = nc.dram_tensor("mixed_kept", (B, DT, P, N), F32, kind="Internal").ap()

        qk_w = sb("qk_w", [P, 2, 2, DT, P], F32R)
        slot_a = sb("slot_a", [P, 2, DT, D], F32R)
        slot_b = sb("slot_b", [P, 2, DT, D], F32R)
        qk_t = sb("qk_t", [P, 2, 2, N], F32R)
        q_stack = sb("q_stack", [P, 2, HG, N], F32R)
        k_stack = sb("k_stack", [P, 2, HG, N], F32R)
        v = sb("v", [P, NT, D])
        xt = sb("xt", [P, 2, DT, N], F32R)
        stage = sb("stage", [P, 4, 512])
        adj_t = sb("adj_t", [P, NT, N])
        x1 = sb("x1", [P, NT, D])
        ot = sb("ot", [P, 2, GROUPS, N], F32R)
        att = sb("att", [P, 4, HG, N])
        pt = sb("pt", [P, HG, NT, 2 * P])
        x1t = sb("x1t", [P, 2, 2, DT, P], F32R)
        sup = sb("sup", [P, 2, NT, D], F32R)
        fold1 = sb("fold1", [P, 256])
        fold2 = sb("fold2", [P, 2, HG, P // 2])
        gam = fold1[:, 0:DT * E].rearrange("p (t e) -> p t e", t=DT)
        bet = fold1[:, DT * E:2 * DT * E].rearrange("p (t e) -> p t e", t=DT)
        bn_raw = sb("bn_raw", [P, B, DT, 6])
        ident = sb("ident", [P, P])
        small = sb("small", [P, 64])
        ones, eps_c = small[:, 0:1], small[:, 1:2]
        rb, iota4 = small[:, 4:8], small[:, 8:12]
        total, live, rinv = small[:, 12:16], small[:, 16:20], small[:, 20:24]
        ln_std, ln_rstd = small[:, 24:28], small[:, 28:32]
        xmean = small[:, 32:36]
        rt = small[:, 40:56].rearrange("p (a e) -> p a e", a=4)
        ln_mv = small[:, 56:64].rearrange("p (t s) -> p t s", s=2)
        rw = sb("rw", [P, DT, E])
        nmax = sb("nmax", [P, 4, HG])
        rsum = sb("rsum", [P, 4, HG])
        ln_raw = sb("ln_raw", [P, NT, 6])
        chosen = sb("chosen", [P, B, E])
        pick = sb("pick", [P, 1], I32)

        s_bank = [pb("s_bank0"), pb("s_bank1")]
        t_bank = [pb("t_bank0"), pb("t_bank1")]
        p_bank = [pb("p_bank0"), pb("p_bank1")]
        o_bank = [pb("o_bank0"), pb("o_bank1")]

        pe = {k: sem("pe_" + k) for k in ("score", "turn", "pv", "Q", "K", "V", "O", "sum", "route", "X", "S", "M")}
        act_pt = sem("act_pt"); act_exp = sem("act_exp"); act_ot = sem("act_ot")
        act_hi = {k: sem("act_hi_" + k) for k in "QKXS"}
        act_v = sem("act_v"); act_mixed = sem("act_mixed"); act_std = sem("act_std")
        act_xt = sem("act_xt"); act_at = sem("act_at")
        dve_logit = sem("dve_logit"); dve_stat = sem("dve_stat"); dve_norm = sem("dve_norm")
        dve_lo = {k: sem("dve_lo_" + k) for k in "QKXS"}
        dve_ot = sem("dve_ot"); dve_y = sem("dve_y"); dve_ln = sem("dve_ln"); dve_pick = sem("dve_pick")
        dve_choice = sem("dve_choice"); dve_applied = sem("dve_applied"); dve_chain = sem("dve_chain")
        dve_x1 = sem("dve_x1"); dve_mean = sem("dve_mean"); dve_route = sem("dve_route")
        dve_bn = sem("dve_bn"); dve_xt = sem("dve_xt"); dve_split = sem("dve_split")
        pool_fold1 = sem("pool_fold1"); pool_halved = sem("pool_halved"); pool_fold2 = sem("pool_fold2"); pool_at = sem("pool_at")
        pool_const = sem("pool_const")
        ld_const = sem("ld_const"); ld_raw = sem("ld_raw"); st_split = sem("st_split")
        ld_qw = sem("ld_qw"); ld_kw = sem("ld_kw"); ld_wv = sem("ld_wv"); ld_wo = sem("ld_wo"); ld_ex = sem("ld_ex")
        ld_xt = sem("ld_xt"); ld_at = sem("ld_at"); ld_x = sem("ld_x")
        ld_adj = [sem(f"ld_adj{t}") for t in range(NT)]
        q_stacked = [sem(f"q_stacked{i}") for i in range(2)]
        k_stacked = [sem(f"k_stacked{i}") for i in range(2)]
        st_x1 = sem("st_x1"); st_mixed = sem("st_mixed")
        dve_bnorm = sem("dve_bnorm"); act_bnorm = sem("act_bnorm")
        f_loadx = [sem(f"f_loadx{i}") for i in range(4)]
        f_loadm = [sem(f"f_loadm{i}") for i in range(4)]
        f_store = [sem(f"f_store{i}") for i in range(4)]
        act_relu = sem("act_relu"); pe_back = sem("pe_back"); dve_res = sem("dve_res")
        dve_fln = sem("dve_fln"); act_fstd = sem("act_fstd"); dve_frstd = sem("dve_frstd"); dve_out = sem("dve_out")

        passed_sp = sem("passed_sp"); passed_dve = sem("passed_dve")

        def wait(eng, s, b, per, more):
            if isinstance(b, int):
                if per * b + more > 0:
                    eng.wait_ge(s, per * b + more)
            else:
                assert per * 2 + more > 0
                eng.wait_ge(s, b * per + more)
                if eng.engine == mybir.EngineType.SP:
                    settle(eng)

        def settle(eng):
            eng.sem_inc(passed_sp if eng.engine == mybir.EngineType.SP else passed_dve, 1)

        def dram(ap, b, off):
            if isinstance(b, int):
                return ap[b + off]
            rest = " ".join(f"d{i}" for i in range(2, len(ap.shape)))
            return ap[bass.ds(b + off, 1)].rearrange(f"a d1 {rest} -> (a d1) {rest}")

        def present(name, has_prev, has_next, attends):
            if name.endswith("-"):
                return has_prev
            if name.endswith("+"):
                return has_next
            return attends

        EMPTIED = {0: -1, 5: 0, 7: 1, 8: 2, 9: 3, 10: 4, 12: 5, 14: 6}
        bank_of = {}
        for k, t in enumerate(TASKS):
            bank_of[t] = k % 2
        assert len(TASKS) % 2 == 0

        def done_by(b, task):
            name, i = task
            k = name[0] if name[0] in "QKVOXSM" else name
            return {
                "Q": (dve_lo["Q"], GROUPS, (i if name == "Q" else GROUPS + i) + 1),
                "K": (dve_lo["K"], GROUPS, (i if name == "K" else GROUPS + i) + 1),
                "V": (act_v, NT, i + 1),
                "O": (dve_y, NT, i + 1 - NT),
                "sum-": (dve_mean, 1, 0),
                "route-": (dve_route, 4, 1 - 4),
                "X": (dve_lo["X"], NT, i + 1 - NT),
                "S": (dve_lo["S"], NT, i + 1 - NT),
                "M": (act_mixed, DT, i + 1 - DT),
            }[k]

        order = TASKS

        def bank_user_before(task, kind, kind_before):
            at = order.index(task)
            for t in reversed(order[:at]):
                if bank_of[t] == bank_of[task] and present(t[0], *kind):
                    return t, 0
            if kind_before is not None:
                for t in reversed(order):
                    if bank_of[t] == bank_of[task] and present(t[0], *kind_before):
                        return t, 1
            return [t for t in AHEAD if bank_of[t] == bank_of[task]][-1], 1

        def wait_bank(eng, b, task, kind, kind_before):
            t, back = bank_user_before(task, kind, kind_before)
            s, per, more = done_by(b, t)
            wait(eng, s, b, per, more - per * back)

        chunks = [(t, c) for t in TASKS for c in range(4)]
        step_chunks, done, allowed = [], 0.0, 0.0
        for step in range(STEPS):
            allowed += HALF_SLOTS[step // 2] / 2
            step_chunks.append([])
            while chunks and (done + 1e-6 < allowed or step == STEPS - 1):
                step_chunks[-1].append(chunks[0])
                done += COST.get(chunks.pop(0)[0][0], 1)

        def plan(u, kind):
            return [[c for c in step_chunks[HG * u + j] if present(c[0][0], *kind)] for j in range(HG)]

        def three_pass(eng, bank, lhs, rhs, kt, last):
            eng.matmul(bank, lhs(0), rhs(0), start=(kt == 0), stop=False)
            eng.matmul(bank, lhs(0), rhs(1), start=False, stop=False)
            return eng.matmul(bank, lhs(1), rhs(0), start=False, stop=last)

        def pe_chunk(eng, b, task, c, kind, kind_before):
            name, i = task
            bank = p_bank[bank_of[task]]
            if c == 0:
                wait_bank(eng, b, task, kind, kind_before)
            if name[0] in "QK":
                which = "QK".index(name[0])
                g = i if not name.endswith("+") else GROUPS + i
                if c == 0:
                    first = sum(t[0] == ("Q+", "K+")[which] for t in AHEAD)
                    wait(eng, (ld_qw, ld_kw)[which], b, GROUPS * 16, (g + 1 - first) * 16)
                    if i == 0:
                        wait(eng, dve_xt, b, DT, 2 * DT)
                        wait(eng, act_xt, b, DT, 2 * DT)
                mm = three_pass(eng, bank[:, :], lambda h: qk_w[:, which, h, c, :], lambda h: xt[:, h, c, :],
                                c, c == DT - 1)
            elif name == "V":
                if c == 0 and i == 0:
                    wait(eng, ld_wv, b, 16, 16)
                mm = three_pass(eng, bank[:, :], lambda h: xt[:, h, c, i * P:(i + 1) * P],
                                lambda h: slot_a[:, h, c, :], c, c == DT - 1)
            elif name == "O-":
                if c == 0 and i == 0:
                    wait(eng, ld_wo, b, 16, 0)
                    wait(eng, dve_ot, b, PAIRS, 0)
                mm = three_pass(eng, bank[:, :], lambda h: ot[:, h, c, i * P:(i + 1) * P],
                                lambda h: slot_b[:, h, c, :], c, c == DT - 1)
            elif name == "sum-":
                if c == 0:
                    wait(eng, dve_x1, b, NT, 0)
                for t in range(NT):
                    mm = eng.matmul(bank[:, c:c + 1], x1[:, t, c * P:(c + 1) * P], ones[:, :],
                                    start=(t == 0), stop=(t == NT - 1))
            elif name == "route-":
                if c == 0:
                    wait(eng, dve_mean, b, 1, 0)
                mm = eng.matmul(bank[:, 0:E], xmean[:, c:c + 1].to_broadcast([P, P]), rw[:, c, :],
                                start=(c == 0), stop=(c == DT - 1))
            elif name == "X-":
                mm = eng.transpose(bank[:, c * P:(c + 1) * P], x1[:, i, c * P:(c + 1) * P], ident[:, :])
            elif name == "S-":
                if c == 0:
                    wait(eng, dve_lo["X"], b, NT, i + 1 - NT)
                    if i == 0:
                        wait(eng, ld_ex, b, 16, 0)
                mm = three_pass(eng, bank[:, :], lambda h: x1t[:, i % 2, h, c, :], lambda h: slot_a[:, h, c, :],
                                c, c == DT - 1)
            else:
                if c == 0 and i == 0:
                    wait(eng, dve_lo["S"], b, NT, 0)
                    wait(eng, pool_at, b, NT, 0)
                mm = three_pass(eng, bank[:, :], lambda h: sup[:, h, c, i * P:(i + 1) * P],
                                lambda h: slot_b[:, h, c, :], c, c == NT - 1)
            if c == 3:
                mm.then_inc(pe[name.rstrip("+-")], 1)

        def wait_stacked(eng, which, b, g):
            wait(eng, (q_stacked, k_stacked)[which][g % 2], b, GROUPS // 2 * 256, (g // 2 + 1) * 256)

        def pe_scores(eng, b, r):
            u, j = divmod(r, HG)
            g, t = divmod(u, NT)
            if j == 0 and t == 0:
                wait_stacked(eng, 0, b, g)
                wait_stacked(eng, 1, b, g)
            wait(eng, dve_logit, b, STEPS, r - 1)
            eng.matmul(s_bank[r % 2][:, :], q_stack[:, g % 2, j, t * P:(t + 1) * P], k_stack[:, g % 2, j, :],
                       start=True, stop=True).then_inc(pe["score"], 1)

        def pe_turn(eng, b, r):
            u, j = divmod(r, HG)
            wait(eng, dve_norm, b, STEPS, r + 1)
            wait(eng, act_pt, b, STEPS, r - 1)
            for m in range(NT):
                mm = eng.transpose(t_bank[r % 2][:, m * P:(m + 1) * P],
                                   att[:, u % 4, j, m * P:(m + 1) * P], ident[:, :])
            mm.then_inc(pe["turn"], 1)

        def pe_pv(eng, b, u):
            pair, g = u // 2, u // NT
            wait(eng, act_pt, b, STEPS, 4 * u + 4)
            wait(eng, dve_ot, b, PAIRS, pair - 1)
            wait(eng, act_v, b, NT, NT)
            for m in range(NT):
                for j in range(HG):
                    head = g * HG + j
                    mm = eng.matmul(o_bank[pair % 2][j * HD:(j + 1) * HD, 0:2 * P],
                                    v[:, m, head * HD:(head + 1) * HD], pt[:, j, m, :],
                                    start=(m == 0), stop=(m == NT - 1), tile_position=(0, j * HD))
            mm.then_inc(pe["pv"], 1)

        def pe_slot(eng, b, u, kind, kind_before):
            attends, has_next = kind[2], kind[1]
            work = plan(u, kind) if u >= 0 else [[]] * HG
            for j in range(HG):
                r = HG * u + j
                if attends and r >= 0:
                    pe_turn(eng, b, r)
                if (attends and r + LEAD < STEPS) or (has_next and r + LEAD >= STEPS):
                    pe_scores(eng, b, r + LEAD)
                for task, c in work[j]:
                    pe_chunk(eng, b, task, c, kind, kind_before)
            if attends and u >= 0 and u % 2 == 1:
                pe_pv(eng, b, u)

        def act_task(eng, b, task, kind):
            name, i = task
            bank = p_bank[bank_of[task]]
            if name[0] in "QK":
                which = "QK".index(name[0])
                g = i if not name.endswith("+") else GROUPS + i
                wait(eng, pe[name[0]], b, GROUPS, g + 1)
                wait_stacked(eng, which, b, g - 1)
                eng.activation(qk_t[:, which, 0, :], bank[:, :], ACT.Copy,
                               scale=HALF_SCALE if which == 0 else 1.0).then_inc(act_hi[name[0]], 1)
            elif name == "V":
                wait(eng, pe["V"], b, NT, i + 1)
                if i == 0:
                    wait(eng, pe["pv"], b, PAIRS, 0)
                eng.activation(v[:, i, :], bank[:, :], ACT.Copy).then_inc(act_v, 1)
            elif name == "X-":
                wait(eng, pe["X"], b, NT, i + 1 - NT)
                wait(eng, pe["S"], b, NT, i - 1 - NT)
                eng.activation(x1t[:, i % 2, 0, :, :].rearrange("p t n -> p (t n)"), bank[:, :],
                               ACT.Copy).then_inc(act_hi["X"], 1)
            elif name == "S-":
                wait(eng, pe["S"], b, NT, i + 1 - NT)
                if i == 0:
                    wait(eng, pe["M"], b, DT, -DT)
                    if isinstance(b, int) and b == 1:
                        eng.wait_ge(st_split, 16 * SPLIT_STORES)
                eng.activation(sup[:, 0, i, :], bank[:, :], ACT.Copy).then_inc(act_hi["S"], 1)
            elif name == "M-":
                wait(eng, pe["M"], b, DT, i + 1 - DT)
                if i == 0:
                    wait(eng, pe["X"], b, NT, 0)
                    wait(eng, st_x1, b, 16, 0)
                eng.activation(x1[:, i, :], bank[:, :], ACT.Copy).then_inc(act_mixed, 1)

        def act_exp_step(eng, b, r):
            u, j = divmod(r, HG)
            wait(eng, dve_logit, b, STEPS, r + 1)
            wait(eng, pool_fold1, b, STEPS, r + 1)
            eng.activation(att[:, u % 4, j, :], att[:, u % 4, j, :], ACT.Exp, bias=nmax[:, u % 4, j:j + 1],
                           scale=-1.0, accum_out=rsum[:, u % 4, j:j + 1]).then_inc(act_exp, 1)

        def act_ot_hi(eng, b, pair):
            g, half = divmod(pair % PAIRS, 2)
            wait(eng, pe["pv"], b, PAIRS, pair + 1)
            if pair == 0:
                wait(eng, pe["O"], b, NT, 2 - NT)
            elif pair == 1:
                wait(eng, pe["O"], b, NT, 0)
            eng.activation(ot[:, 0, g, half * 256:half * 256 + 256], o_bank[pair % 2][:, 0:256],
                           ACT.Copy).then_inc(act_ot, 1)

        def act_slot(eng, b, u, kind, kind_before):
            has_prev, has_next, attends = kind
            work = plan(u, kind) if u >= 0 else [[]] * HG
            for j in range(HG):
                if j == 1 and u in EMPTIED and (attends if u else has_prev):
                    act_ot_hi(eng, b, EMPTIED[u])
                if u == 8 and has_prev:
                    if j == 0:
                        wait(eng, pe["O"], b, NT, 0)
                        wait(eng, ld_at, b, 16, 0)
                    eng.activation(slot_b[:, 0, j, :], stage[:, j, :], ACT.Copy).then_inc(act_at, 1)
                if u == 6 and j == 3 and has_prev:
                    wait(eng, dve_ln, b, 8, 0)
                    eng.activation(ln_std[:, :], ln_mv[:, :, 1], ACT.Sqrt, bias=eps_c[:, :]).then_inc(act_std, 1)
                if u == 6 and has_next:
                    if j == 0:
                        wait(eng, pe["K"], b, GROUPS, GROUPS)
                        wait(eng, pe["Q"], b, GROUPS, GROUPS)
                        wait(eng, ld_xt, b, 16, 32)
                    eng.activation(xt[:, 0, j, :], stage[:, j, :], ACT.Copy).then_inc(act_xt, 1)
                r = HG * u + j
                if attends and r >= 0:
                    wait(eng, pe["turn"], b, STEPS, r + 1)
                    if u % 2 == 0 and j == 0:
                        wait(eng, pe["pv"], b, PAIRS, u // 2)
                    eng.activation(pt[:, j, :, (u % 2) * P:(u % 2 + 1) * P],
                                   t_bank[r % 2][:, :].rearrange("p (m n) -> p m n", m=NT),
                                   ACT.Copy).then_inc(act_pt, 1)
                e = r + EXP_LEAD
                if e >= 0 and ((attends and e < STEPS) or (has_next and e >= STEPS)):
                    act_exp_step(eng, b, e)
                for task, c in work[j]:
                    if c == 3:
                        act_task(eng, b, task, kind)

        def dve_logits(eng, b, r):
            u, j = divmod(r, HG)
            t = u % NT
            wait(eng, pe["score"], b, STEPS, r + 1)
            if j == 0:
                if u % UNITS < NT:
                    wait(eng, ld_adj[t], b, 16, 16 * (1 + u // UNITS))
                wait(eng, pe["turn"], b, STEPS, 4 * (u - 4) + 4)
            if not isinstance(b, int):
                settle(eng)
            eng.tensor_tensor_reduce(out=att[:, u % 4, j, :], in0=s_bank[r % 2][:, :], in1=adj_t[:, t, :],
                                     scale=-2.0, scalar=3.0e38, op0=ALU.add, op1=ALU.min,
                                     accum_out=nmax[:, u % 4, j:j + 1]).then_inc(dve_logit, 1)

        def dve_total(eng, b, u):
            wait(eng, pool_fold2, b, STEPS, HG * (u + 1))
            wait(eng, dve_stat, b, 3 * UNITS, 3 * u)
            eng.tensor_reduce(total[:, :], fold2[:, u % 2, :, :], AX.X, ALU.add).then_inc(dve_stat, 1)

        def dve_live(eng, b, u):
            wait(eng, dve_norm, b, STEPS, HG * u)
            wait(eng, dve_logit, b, STEPS, HG * (u + 1))
            wait(eng, dve_stat, b, 3 * UNITS, 3 * u + 1)
            eng.scalar_tensor_tensor(out=live[:, :], in0=total[:, :], scalar=0.0, in1=nmax[:, u % 4, :],
                                     op0=ALU.not_equal, op1=ALU.logical_or).then_inc(dve_stat, 1)

        def dve_reciprocal(eng, b, u):
            wait(eng, act_exp, b, STEPS, HG * (u + 1))
            eng.reciprocal(rinv[:, :], rsum[:, u % 4, :]).then_inc(dve_stat, 1)
            wait(eng, dve_stat, b, 3 * UNITS, 3 * u + 3)

        def dve_normalise(eng, b, r):
            u, j = divmod(r, HG)
            eng.tensor_scalar(att[:, u % 4, j, :], att[:, u % 4, j, :], rinv[:, j:j + 1], live[:, j:j + 1],
                              ALU.mult, ALU.mult).then_inc(dve_norm, 1)

        def dve_low(eng, dst, src, hi, scale=1.0):
            if scale == 1.0:
                return eng.tensor_tensor(dst, src, hi.bitcast(F32), ALU.subtract)
            return eng.scalar_tensor_tensor(out=dst, in0=src, scalar=scale, in1=hi.bitcast(F32), op0=ALU.mult,
                                            op1=ALU.subtract)

        def dve_task(eng, b, task, kind):
            name, i = task
            bank = p_bank[bank_of[task]]
            if name[0] in "QK":
                which = "QK".index(name[0])
                g = i if not name.endswith("+") else GROUPS + i
                wait(eng, act_hi[name[0]], b, GROUPS, g + 1)
                dve_low(eng, qk_t[:, which, 1, :], bank[:, :], qk_t[:, which, 0, :],
                        HALF_SCALE if which == 0 else 1.0).then_inc(dve_lo[name[0]], 1)
            elif name == "O-":
                wait(eng, pe["O"], b, NT, i + 1 - NT)
                wait(eng, ld_x, b, 16, 0)
                eng.tensor_tensor(x1[:, i, :], bank[:, :], x1[:, i, :], ALU.add).then_inc(dve_y, 1)
                wait(eng, dve_y, b, NT, i + 1 - NT)
                eng.bn_stats(ln_raw[:, i, :], x1[:, i, :]).then_inc(dve_ln, 1)
                wait(eng, dve_ln, b, 8, 2 * i + 1 - 8)
                settle(eng)
                eng.bn_aggr(ln_mv[:, i, :], ln_raw[:, i, :]).then_inc(dve_ln, 1)
            elif name == "sum-":
                wait(eng, pe["sum"], b, 1, 0)
                eng.tensor_scalar(xmean[:, :], bank[:, 0:DT], 1.0 / N, None, ALU.mult).then_inc(dve_mean, 1)
            elif name == "route-":
                wait(eng, pe["route"], b, 1, 0)
                eng.tensor_tensor(rt[:, 0, :], bank[:, 0:E], rb[:, :], ALU.add).then_inc(dve_route, 1)
                wait(eng, dve_route, b, 4, -3)
                eng.tensor_reduce(rt[:, 1, 0:1], rt[:, 0, :], AX.X, ALU.max).then_inc(dve_route, 1)
                wait(eng, dve_route, b, 4, -2)
                eng.tensor_scalar(rt[:, 2, :], rt[:, 0, :], rt[:, 1, 0:1], -float(E), ALU.is_ge,
                                  ALU.mult).then_inc(dve_route, 1)
                wait(eng, dve_route, b, 4, -1)
                eng.tensor_tensor(rt[:, 3, :], rt[:, 2, :], iota4[:, :], ALU.add).then_inc(dve_route, 1)
            elif name in ("X-", "S-"):
                k = name[0]
                wait(eng, act_hi[k], b, NT, i + 1 - NT)
                if k == "X":
                    dve_low(eng, x1t[:, i % 2, 1, :, :].rearrange("p t n -> p (t n)"), bank[:, :],
                            x1t[:, i % 2, 0, :, :].rearrange("p t n -> p (t n)")).then_inc(dve_lo["X"], 1)
                else:
                    dve_low(eng, sup[:, 1, i, :], bank[:, :], sup[:, 0, i, :]).then_inc(dve_lo["S"], 1)
            elif name == "M-":
                wait(eng, act_mixed, b, DT, i + 1 - DT)
                row = slice(b - 1, b) if isinstance(b, int) else bass.ds(b - 1, 1)
                eng.bn_stats(bn_raw[:, row, i, :].rearrange("p o s -> p (o s)"), x1[:, i, :]).then_inc(dve_bn, 1)

        def dve_choose(eng, b):
            wait(eng, dve_route, b, 4, 0)
            eng.tensor_reduce(rt[:, 1, 1:2], rt[:, 3, :], AX.X, ALU.min).then_inc(dve_pick, 1)
            wait(eng, dve_pick, b, 3, -2)
            eng.tensor_scalar(pick[:, :], rt[:, 1, 1:2], float(E), float(E - 1), ALU.add,
                              ALU.min).then_inc(dve_pick, 1)
            eng.tensor_scalar(rt[:, 2, :], iota4[:, :], float(E), None, ALU.subtract).then_inc(dve_pick, 1)
            wait(eng, dve_pick, b, 3, 0)
            row = slice(b - 1, b) if isinstance(b, int) else bass.ds(b - 1, 1)
            eng.tensor_scalar(chosen[:, row, :], rt[:, 2:3, :], rt[:, 1, 1:2], None,
                              ALU.is_equal).then_inc(dve_choice, 1)

        def dve_slot(eng, b, u, kind, kind_before):
            has_prev, has_next, attends = kind
            work = plan(u, kind) if u >= 0 else [[]] * HG
            for j in range(HG):
                if j == 2 and u in EMPTIED and (attends if u else has_prev):
                    pair = EMPTIED[u]
                    g, half = divmod(pair % PAIRS, 2)
                    wait(eng, act_ot, b, PAIRS, pair + 1)
                    dve_low(eng, ot[:, 1, g, half * 256:half * 256 + 256], o_bank[pair % 2][:, 0:256],
                            ot[:, 0, g, half * 256:half * 256 + 256]).then_inc(dve_ot, 1)
                if u == 6 and has_next:
                    wait(eng, act_xt, b, DT, DT + j + 1)
                    dve_low(eng, xt[:, 1, j, :], stage[:, j, :], xt[:, 0, j, :]).then_inc(dve_xt, 1)
                r = HG * u + j
                ahead = u + NORM_UNITS
                starts = ahead >= 0 and (attends if ahead < UNITS else has_next)
                goes_on = ahead - 1 >= 0 and (attends if ahead - 1 < UNITS else has_next)
                if starts and j == 2:
                    dve_live(eng, b, ahead)
                if (attends and r + LEAD < STEPS) or (has_next and r + LEAD >= STEPS):
                    dve_logits(eng, b, r + LEAD)
                if starts and j == 1:
                    dve_total(eng, b, ahead)
                if starts and j == 2:
                    dve_reciprocal(eng, b, ahead)
                if j < 2 and goes_on:
                    dve_normalise(eng, b, HG * (ahead - 1) + 2 + j)
                if j >= 2 and starts:
                    dve_normalise(eng, b, HG * ahead + j - 2)
                if (u, j) in ((6, 3), (7, 0)) and has_prev:
                    if j == 3:
                        wait(eng, act_std, b, 1, 0)
                        eng.reciprocal(ln_rstd[:, :], ln_std[:, :]).then_inc(dve_applied, 1)
                        wait(eng, dve_applied, b, 1, 0)
                    for t in (0, 1) if j == 3 else (2, 3):
                        eng.tensor_scalar(x1[:, t, :], x1[:, t, :], ln_mv[:, t, 0:1], ln_rstd[:, t:t + 1],
                                          ALU.subtract, ALU.mult).then_inc(dve_x1, 1)
                for task, c in work[j]:
                    if c == 3:
                        dve_task(eng, b, task, kind)
                        if task[0] == "route-":
                            dve_choose(eng, b)

        def pool_slot(eng, b, u, kind, kind_before):
            has_prev, has_next, attends = kind
            for j in range(HG):
                r = HG * u + j + LEAD
                if (attends and r < STEPS) or (has_next and r >= STEPS):
                    uu, jj = divmod(r, HG)
                    wait(eng, dve_logit, b, STEPS, r + 1)
                    wait(eng, pool_fold2, b, STEPS, r)
                    a = att[:, uu % 4, jj, :]
                    eng.tensor_tensor(fold1[:, :], a[:, 0:256], a[:, 256:512], ALU.add).then_inc(pool_fold1, 1)
                    wait(eng, pool_fold1, b, STEPS, r + 1)
                    eng.tensor_tensor(fold1[:, 0:P], fold1[:, 0:P], fold1[:, P:2 * P],
                                      ALU.add).then_inc(pool_halved, 1)
                    wait(eng, pool_halved, b, STEPS, r + 1)
                    if jj == 0:
                        wait(eng, dve_stat, b, 3 * UNITS, 3 * (uu - 2) + 1)
                    eng.tensor_tensor(fold2[:, uu % 2, jj, :], fold1[:, 0:P // 2], fold1[:, P // 2:P],
                                      ALU.add).then_inc(pool_fold2, 1)
            for t in (0, 1) if u == 8 else (2, 3) if u == 9 else ():
                if not has_prev:
                    break
                if t == 0:
                    wait(eng, act_at, b, NT, 0)
                eng.tensor_tensor(slot_b[:, 1, t, :], stage[:, t, :], slot_b[:, 0, t, :].bitcast(F32),
                                  ALU.subtract).then_inc(pool_at, 1)

        def stack(eng, b, which, g):
            src_sem_hi, src_sem_lo = act_hi["QK"[which]], dve_lo["QK"[which]]
            wait(eng, src_sem_hi, b, GROUPS, g + 1)
            wait(eng, src_sem_lo, b, GROUPS, g + 1)
            wait(eng, pe["score"], b, STEPS, NT * HG * (g - 1))
            dst = (q_stack, k_stack)[which][:, g % 2]
            done = (q_stacked, k_stacked)[which][g % 2]
            for block in range(4):
                part = block // 2 if which == 0 else block % 2
                for j in range(HG):
                    eng.dma_start(dst[block * HD:(block + 1) * HD, j, :].bitcast(F32),
                                  qk_t[j * HD:(j + 1) * HD, which, part, :].bitcast(F32)).then_inc(done, 16)

        def load_qk_w(eng, b, which, g):
            wait(eng, pe["QK"[which]], b, GROUPS, g)
            eng.dma_start(qk_w[:, which].bitcast(F32), qk_dram[which, g % GROUPS]).then_inc((ld_qw, ld_kw)[which], 16)

        def sp_slot(eng, b, u, kind, kind_before):
            has_prev, has_next, attends = kind
            if u == 0 and has_prev:
                wait(eng, pe["M"], b, DT, -DT)
                if isinstance(b, int) and b == 1:
                    eng.wait_ge(st_split, 16 * SPLIT_STORES)
                eng.dma_start(slot_b[:].bitcast(F32), vo_dram[1]).then_inc(ld_wo, 16)
                wait(eng, st_mixed, b, 16 * DT, -16 * DT)
                wait(eng, dve_bn, b, DT, -DT)
                eng.dma_start(x1[:, :, :], dram(x, b, -1).rearrange("(t p) n -> p t n", p=P)).then_inc(ld_x, 16)
            if u == 0 and has_next:
                wait(eng, pool_at, b, NT, -NT)
                wait(eng, act_at, b, NT, -NT)
                wait(eng, act_xt, b, DT, DT)
                wait(eng, dve_xt, b, DT, DT)
                eng.dma_start(stage[:, :, :], dram(xT, b, 1).rearrange("(t p) n -> p t n", p=P)).then_inc(ld_xt, 16)
            if u == 1 and attends:
                stack(eng, b, 0, 2)
            if u == 2 and attends:
                load_qk_w(eng, b, 1, 3)
                stack(eng, b, 1, 2)
            if u == 4 and attends:
                if has_next:
                    load_qk_w(eng, b, 0, 4)
                stack(eng, b, 0, 3)
            if u == 5 and attends:
                if has_next:
                    load_qk_w(eng, b, 1, 4)
                stack(eng, b, 1, 3)
            if u == 7 and has_prev:
                wait(eng, act_xt, b, DT, (1 + has_next) * DT if attends else 0)
                wait(eng, dve_xt, b, DT, (1 + has_next) * DT if attends else 0)
                eng.dma_start(stage[:, :, :], dram(adjT, b, -1).rearrange("(t p) n -> p t n", p=P))\
                    .then_inc(ld_at, 16)
                wait(eng, dve_x1, b, NT, 0)
                eng.dma_start(dram(x1_dram, b, -1).rearrange("t p n -> p t n"), x1[:, :, :]).then_inc(st_x1, 16)
            if u == 7 and has_next:
                load_qk_w(eng, b, 0, 5)
            if u == 8 and has_prev:
                wait(eng, dve_pick, b, 3, -1)
                if attends:
                    wait(eng, pe["V"], b, NT, NT)
                else:
                    wait(eng, pe["S"], b, NT, -NT)
                e = eng.value_load(pick[0:1, 0:1], min_val=0, max_val=E - 1)
                eng.dma_start(slot_a[:].bitcast(F32),
                              ex_dram[bass.ds(e, 1)].rearrange("a p h t n -> (a p) h t n")).then_inc(ld_ex, 16)
            if u == 8 and has_next:
                stack(eng, b, 0, 4)
            if u == 9 and has_next:
                load_qk_w(eng, b, 1, 5)
                stack(eng, b, 1, 4)
            if 10 <= u <= 13 and has_next:
                t = u - 10
                wait(eng, dve_logit, b, STEPS, HG * (3 * NT + t + 1))
                eng.dma_start(adj_t[:, t, :], dram(adj, b, 1)[t * P:(t + 1) * P, :]).then_inc(ld_adj[t], 16)
            if u == 12 and has_next:
                wait(eng, pe["S"], b, NT, 0)
                if not has_prev:
                    wait(eng, pe["V"], b, NT, NT)
                eng.dma_start(slot_a[:].bitcast(F32), vo_dram[0]).then_inc(ld_wv, 16)
                load_qk_w(eng, b, 0, 6)
                stack(eng, b, 0, 5)
            if u == 13 and has_next:
                load_qk_w(eng, b, 1, 6)
                stack(eng, b, 1, 5)
            for i in {13: (0,), 14: (1,), 15: (2, 3)}.get(u, ()) if has_prev else ():
                wait(eng, act_mixed, b, DT, i + 1 - DT)
                eng.dma_start(dram(mixed_dram, b, -1)[i], x1[:, i, :]).then_inc(st_mixed, 16)
            if u == 15 and has_next:
                load_qk_w(eng, b, 0, 7)

        raw_buf = [att[:, 0], att[:, 1]]
        hilo_buf = [sup, ot, slot_b]
        early = [by_tile(wqT), by_tile(wkT)]
        late = [by_tile(woT)] + [by_tile(experts[e]) for e in range(E)]
        sup_w = sup[:].bitcast(F32)
        SPLIT_STORES = 4 + 4 + 1 + 1 + E

        def dve_split_weights(eng, raw, hilo, n):
            eng.tensor_copy(hilo[:, 0].bitcast(F32R), raw).then_inc(dve_split, 1)
            eng.wait_ge(dve_split, 2 * n + 1)
            eng.tensor_tensor(hilo[:, 1].bitcast(F32R), raw, hilo[:, 0], ALU.subtract).then_inc(dve_split, 1)

        FIRST, MID, LAST, TAIL = (False, True, True), (True, True, True), (True, False, True), (True, False, False)

        def graphs(eng, slot, ahead=None, in_first=None):
            for u in range(-(LEAD // HG), 0):
                slot(eng, 0, u, FIRST, None)
            for u in range(UNITS):
                slot(eng, 0, u, FIRST, None)
                if in_first:
                    in_first(u)
            for u in range(UNITS):
                slot(eng, 1, u, MID, FIRST)
            with eng.Fori(2, B - 1) as b:
                for u in range(UNITS):
                    slot(eng, b, u, MID, MID)
            for u in range(UNITS):
                slot(eng, B - 1, u, LAST, MID)
            for u in range(UNITS):
                slot(eng, B, u, TAIL, LAST)

        y_buf = [att[:, i] for i in range(4)]
        z_buf = [stage, adj_t, x1, v]
        back_bank = [p_bank[0], p_bank[1], t_bank[0], t_bank[1], s_bank[0], s_bank[1], o_bank[0], o_bank[1]]
        bn_all = fold2[:, :].rearrange("p a b c -> p (a b c)")
        bn_s = bn_all[:, 0:2 * B * DT].rearrange("p (s b t) -> p s b t", s=2, b=B)
        tmp = bn_all[:, P:4 * P]
        bn_tmp = tmp[:, 0:B * DT].rearrange("p (b t) -> p b t", b=B)
        bn_sum = tmp[:, 64:64 + 2 * E * DT].rearrange("p (s e t) -> p s e t", s=2, e=E)
        bn_cnt = tmp[:, 96:96 + E]
        bn_scale = tmp[:, 128:128 + E * DT].rearrange("p (e t) -> p e t", e=E)
        bn_shift = tmp[:, 144:144 + E * DT].rearrange("p (e t) -> p e t", e=E)
        bn_w1 = tmp[:, 160:160 + E * DT].rearrange("p (e t) -> p e t", e=E)
        g_scale = tmp[:, 192:192 + B * DT].rearrange("p (b t) -> p b t", b=B)
        g_shift = tmp[:, 256:256 + B * DT].rearrange("p (b t) -> p b t", b=B)
        bn_tmp2 = tmp[:, 320:320 + B * DT].rearrange("p (b t) -> p b t", b=B)

        block = ctx.enter_context(nc.Block())

        @block.sync
        def _(sp):
            sp.dma_start(raw_buf[0], early[0]).then_inc(ld_raw, 16)
            sp.dma_start(stage[:, :, :], xT[0].rearrange("(t p) n -> p t n", p=P)).then_inc(ld_xt, 16)
            sp.wait_ge(ld_raw, 16)
            sp.dma_start(raw_buf[1], early[1]).then_inc(ld_raw, 16)
            sp.dma_start(rw[:, :, :], router_w.rearrange("(t p) e -> p t e", p=P)).then_inc(ld_const, 16)
            sp.dma_start(rb[:, :], router_b[0:1, :].to_broadcast([P, E])).then_inc(ld_const, 16)
            sp.wait_ge(ld_raw, 32)
            sp.dma_start(x1[:, :, :], by_tile(wvT)).then_inc(ld_raw, 16)
            for t in range(NT):
                sp.dma_start(adj_t[:, t, :], adj[0, t * P:(t + 1) * P, :]).then_inc(ld_adj[t], 16)
            stack(sp, 0, 0, 0)
            stack(sp, 0, 1, 0)
            for which in range(2):
                sp.wait_ge(dve_split, 2 * (which + 1))
                for g in range(GROUPS):
                    sp.dma_start(qk_dram[which, g],
                                 hilo_buf[which][:, :, :, g * P:(g + 1) * P].bitcast(F32)).then_inc(st_split, 16)
            sp.wait_ge(dve_split, 6)
            sp.dma_start(vo_dram[0], slot_b[:].bitcast(F32)).then_inc(st_split, 16)
            stack(sp, 0, 0, 1)
            stack(sp, 0, 1, 1)
            sp.wait_ge(st_split, 16 * 9)
            sp.dma_start(slot_a[:].bitcast(F32), vo_dram[0]).then_inc(ld_wv, 16)
            load_qk_w(sp, 0, 1, 2)
            load_qk_w(sp, 0, 0, 3)

            def late_weights(u):
                if u in SPLIT_SLOTS:
                    n = SPLIT_SLOTS[u]
                    if n == 0:
                        sp.dma_start(x1[:, :, :], late[0]).then_inc(ld_raw, 16)
                    sp.wait_ge(dve_split, 6 + 2 * (n + 1))
                    sp.dma_start(vo_dram[1] if n == 0 else ex_dram[n - 1], sup_w).then_inc(st_split, 16)
                    if n + 1 < len(late):
                        sp.dma_start(x1[:, :, :], late[n + 1]).then_inc(ld_raw, 16)
            graphs(sp, sp_slot, in_first=late_weights)

            sp.wait_ge(pool_fold2, B * STEPS)
            sp.dma_start(gam[:, :, :], gammaT.rearrange("(t p) e -> p t e", p=P)).then_inc(ld_const, 16)
            sp.dma_start(bet[:, :, :], betaT.rearrange("(t p) e -> p t e", p=P)).then_inc(ld_const, 16)
            sp.wait_ge(st_x1, 16 * B)
            sp.wait_ge(st_mixed, 16 * DT * B)
            sp.wait_ge(act_mixed, DT * B)
            sp.wait_ge(dve_bn, DT * B)
            for i in range(4):
                sp.dma_start(y_buf[i], mixed_dram[i].rearrange("t p n -> p t n")).then_inc(f_loadm[i], 16)
                sp.dma_start(z_buf[i][:, :, :], x1_dram[i].rearrange("t p n -> p t n")).then_inc(f_loadx[i], 16)

            def mixed_next(k, i):
                wait(sp, pe_back, k, 4 * NT, NT * (i + 1))
                sp.dma_start(y_buf[i], dram(mixed_dram, 4 * k, i + 4).rearrange("t p n -> p t n"))\
                    .then_inc(f_loadm[i], 16)

            def store(k, i):
                wait(sp, dve_out, k, 4 * NT, NT * (i + 1))
                sp.dma_start(dram(out, 4 * k, i).rearrange("(t p) n -> p t n", p=P), z_buf[i][:, :, :])\
                    .then_inc(f_store[i], 16)

            def x1_next(k, i):
                wait(sp, f_store[i], k, 16, 16)
                sp.dma_start(z_buf[i][:, :, :], dram(x1_dram, 4 * k, i + 4).rearrange("t p n -> p t n"))\
                    .then_inc(f_loadx[i], 16)
            rounds = B // 4
            for i in range(4):
                mixed_next(0, i)
                store(0, i)
                if i:
                    x1_next(0, i - 1)
            with sp.Fori(1, rounds - 1) as k:
                for i in range(4):
                    mixed_next(k, i)
                    store(k, i)
                    x1_next(k - 1 if i == 0 else k, (i - 1) % 4)
            x1_next(rounds - 2, 3)
            for i in range(4):
                store(rounds - 1, i)
            for i in range(4):
                sp.wait_ge(f_store[i], 16 * rounds)

        @block.gpsimd
        def _(pool):
            pool.memset(ident[:, :], 0.0).then_inc(pool_const, 1)
            pool.memset(ones[:, :], 1.0).then_inc(pool_const, 1)
            pool.memset(eps_c[:, :], EPS).then_inc(pool_const, 1)
            for e in range(E):
                pool.memset(iota4[:, e:e + 1], float(e)).then_inc(pool_const, 1)
            pool.wait_ge(pool_const, 3 + E)
            pool.affine_select(out=ident[:, :], in_=ident[:, :], compare_op=ALU.not_equal, fill=1.0, base=0,
                               pattern=[[-1, P]], channel_multiplier=1).then_inc(pool_const, 1)
            graphs(pool, pool_slot)

        @block.scalar
        def _(act):
            act.wait_ge(pool_const, 4 + E)
            act.wait_ge(ld_xt, 16)
            act.activation(xt[:, 0, :, :], stage[:, :, :], ACT.Copy).then_inc(act_xt, DT)
            for task in AHEAD:
                act_task(act, -1, task, FIRST)
            act.wait_ge(st_split, 16 * 9)
            graphs(act, act_slot)
            act.wait_ge(dve_bnorm, 1)
            act.activation(bn_w1, bn_w1, ACT.Sqrt, bias=eps_c[:, :]).then_inc(act_bnorm, 1)

            def relu(b, i):
                for t in range(DT):
                    at = slice(b + i, b + i + 1) if isinstance(b, int) else bass.ds(b + i, 1)
                    act.activation(y_buf[i % 4][:, t, :], y_buf[i % 4][:, t, :], ACT.Relu,
                                   bias=g_shift[:, at, t], scale=g_scale[:, at, t]).then_inc(act_relu, 1)

            def deviation(count):
                act.wait_ge(dve_fln, count)
                act.activation(ln_std[:, :], ln_mv[:, :, 1], ACT.Sqrt, bias=eps_c[:, :]).then_inc(act_fstd, 1)

            act.wait_ge(dve_bnorm, 2)
            act.wait_ge(f_loadm[0], 16)
            relu(0, 0)
            with act.Fori(0, B // 4 - 1) as k:
                for i in range(4):
                    act.wait_ge(f_loadm[(i + 1) % 4], k * 16 + (16 if i < 3 else 32))
                    relu(k * 4, i + 1)
                    deviation(k * (8 * NT) + 2 * NT * (i + 1))
            for i in range(4):
                if i < 3:
                    act.wait_ge(f_loadm[i + 1], 16 * (B // 4))
                    relu(B - 4, i + 1)
                deviation(2 * NT * (B - 4 + i + 1))

        @block.vector
        def _(dve):
            dve.wait_ge(ld_raw, 16)
            dve_split_weights(dve, raw_buf[0], sup_w, 0)
            dve.wait_ge(act_xt, DT)
            dve_low(dve, xt[:, 1, :, :], stage[:, :, :], xt[:, 0, :, :]).then_inc(dve_xt, DT)
            dve.wait_ge(ld_raw, 32)
            dve_split_weights(dve, raw_buf[1], ot[:].bitcast(F32), 1)
            for task in AHEAD[:2]:
                dve_task(dve, -1, task, FIRST)
            dve.wait_ge(ld_raw, 48)
            dve_split_weights(dve, x1[:, :, :], slot_b[:].bitcast(F32), 2)
            for task in AHEAD[2:]:
                dve_task(dve, -1, task, FIRST)
            dve.wait_ge(st_split, 16 * 9)
            dve.wait_ge(pool_const, 4 + E)
            dve.wait_ge(ld_const, 32)

            def late_weights(u):
                if u in SPLIT_SLOTS:
                    n = SPLIT_SLOTS[u]
                    dve.wait_ge(ld_raw, 16 * (3 + n + 1))
                    dve.wait_ge(st_split, 16 * (9 + n))
                    dve_split_weights(dve, x1[:, :, :], sup_w, 3 + n)
            graphs(dve, dve_slot, in_first=late_weights)

            chain = [0]

            def link(ins):
                chain[0] += 1
                ins.then_inc(dve_chain, 1)
                dve.wait_ge(dve_chain, chain[0])
            dve.wait_ge(ld_const, 64)
            dve.wait_ge(dve_bn, DT * B)
            dve.wait_ge(dve_choice, B)
            sums, squares = bn_s[:, 0], bn_s[:, 1]
            even, odd = bn_raw[:, :, :, 1], bn_raw[:, :, :, 4]
            half = float(N // 2)
            link(dve.tensor_tensor(sums, even, odd, ALU.add))
            link(dve.tensor_scalar(sums, sums, half, None, ALU.mult))
            link(dve.tensor_tensor(squares, even, even, ALU.mult))
            link(dve.tensor_tensor(bn_tmp, odd, odd, ALU.mult))
            link(dve.tensor_tensor(squares, squares, bn_tmp, ALU.add))
            link(dve.tensor_scalar(squares, squares, half, None, ALU.mult))
            link(dve.tensor_tensor(squares, squares, bn_raw[:, :, :, 2], ALU.add))
            link(dve.tensor_tensor(squares, squares, bn_raw[:, :, :, 5], ALU.add))
            for e in range(E):
                hot = chosen[:, :, e:e + 1].to_broadcast([P, B, DT])
                link(dve.tensor_reduce(bn_cnt[:, e:e + 1], chosen[:, :, e], AX.X, ALU.add))
                for s in range(2):
                    link(dve.tensor_tensor(bn_tmp, bn_s[:, s], hot, ALU.mult))
                    link(dve.tensor_reduce(bn_sum[:, s, e, :], bn_tmp.rearrange("p b t -> p t b"), AX.X, ALU.add))
            link(dve.tensor_scalar(bn_cnt, bn_cnt, float(N), 1.0, ALU.mult, ALU.max))
            link(dve.reciprocal(bn_cnt, bn_cnt))
            for s in range(2):
                link(dve.tensor_tensor(bn_sum[:, s], bn_sum[:, s],
                                       bn_cnt.rearrange("p (e o) -> p e o", o=1).to_broadcast([P, E, DT]), ALU.mult))
            link(dve.tensor_tensor(bn_w1, bn_sum[:, 0], bn_sum[:, 0], ALU.mult))
            dve.tensor_tensor(bn_w1, bn_sum[:, 1], bn_w1, ALU.subtract).then_inc(dve_bnorm, 1)
            dve.wait_ge(act_bnorm, 1)
            link(dve.reciprocal(bn_w1, bn_w1))
            link(dve.tensor_tensor(bn_scale, bn_w1, gam[:, :, :].rearrange("p t e -> p e t"), ALU.mult))
            link(dve.tensor_tensor(bn_w1, bn_sum[:, 0], bn_scale, ALU.mult))
            link(dve.tensor_tensor(bn_shift, bet[:, :, :].rearrange("p t e -> p e t"), bn_w1, ALU.subtract))
            for dst, src in ((g_scale, bn_scale), (g_shift, bn_shift)):
                for e in range(E):
                    hot = chosen[:, :, e:e + 1].to_broadcast([P, B, DT])
                    val = src[:, e:e + 1, :].to_broadcast([P, B, DT])
                    if e == 0:
                        link(dve.tensor_tensor(dst, hot, val, ALU.mult))
                    else:
                        link(dve.tensor_tensor(bn_tmp2, hot, val, ALU.mult))
                        link(dve.tensor_tensor(dst, dst, bn_tmp2, ALU.add))
            dve.tensor_scalar(bn_tmp2, bn_tmp2, 0.0, None, ALU.mult).then_inc(dve_bnorm, 1)
            dve.wait_ge(dve_bnorm, 2)
            dve.tensor_scalar(bn_tmp2, bn_tmp2, 0.0, None, ALU.mult).then_inc(dve_res, 8)

            with dve.Fori(0, B // 4) as k:
                for i in range(4):
                    z = z_buf[i]
                    dve.wait_ge(f_loadx[i], k * 16 + 16)
                    for t in range(NT):
                        dve.wait_ge(pe_back, k * (4 * NT) + NT * i + t + 1)
                        dve.tensor_tensor(z[:, t, :], back_bank[(NT * i + t) % 8][:, :], z[:, t, :],
                                          ALU.add).then_inc(dve_res, 1)
                        dve.wait_ge(dve_res, k * (4 * NT) + 8 + NT * i + t + 1)
                        dve.bn_stats(ln_raw[:, t, :], z[:, t, :]).then_inc(dve_fln, 1)
                        dve.wait_ge(dve_fln, k * (8 * NT) + 2 * (NT * i + t) + 1)
                        settle(dve)
                        dve.bn_aggr(ln_mv[:, t, :], ln_raw[:, t, :]).then_inc(dve_fln, 1)
                    dve.wait_ge(act_fstd, k * 4 + i + 1)
                    dve.reciprocal(ln_rstd[:, :], ln_std[:, :]).then_inc(dve_frstd, 1)
                    dve.wait_ge(dve_frstd, k * 4 + i + 1)
                    for t in range(NT):
                        dve.tensor_scalar(z[:, t, :], z[:, t, :], ln_mv[:, t, 0:1], ln_rstd[:, t:t + 1],
                                          ALU.subtract, ALU.mult).then_inc(dve_out, 1)

        @block.tensor
        def _(eng):
            eng.wait_ge(pool_const, 4 + E)
            eng.wait_ge(ld_const, 32)
            for n, task in enumerate(AHEAD):
                earlier = [t for t in AHEAD[:n] if bank_of[t] == bank_of[task]]
                if earlier:
                    s, per, more = done_by(-1, earlier[-1])
                    wait(eng, s, -1, per, more)
                which = "QK".index(task[0][0])
                eng.wait_ge(dve_split, 2 * (which + 1))
                eng.wait_ge(act_xt, DT)
                eng.wait_ge(dve_xt, DT)
                for c in range(DT):
                    mm = three_pass(eng, p_bank[bank_of[task]][:, :], 
                                    lambda h: hilo_buf[which][:, h, c, task[1] * P:(task[1] + 1) * P],
                                    lambda h: xt[:, h, c, :], c, c == DT - 1)
                mm.then_inc(pe[task[0][0]], 1)
            graphs(eng, pe_slot)
            with eng.Fori(0, B // 4) as k:
                for i in range(4):
                    eng.wait_ge(act_relu, k * (4 * DT) + DT * (i + 1))
                    for t in range(NT):
                        eng.wait_ge(dve_res, k * (4 * NT) + NT * i + t + 1)
                        for c in range(DT):
                            mm = eng.transpose(back_bank[(NT * i + t) % 8][:, c * P:(c + 1) * P],
                                               y_buf[i][:, c, t * P:(t + 1) * P], ident[:, :])
                        mm.then_inc(pe_back, 1)


_OUT = (16, 512, 512)


def kernel(**inputs):
    import numpy as np
    import concourse.bacc as bacc
    from concourse.bass_utils import run_bass_kernel_spmd

    def flip(a):
        return np.ascontiguousarray(np.swapaxes(np.asarray(a), -1, -2))

    x, adj = inputs["x"], inputs["adj"]
    laid = [
        ("x", np.ascontiguousarray(x)), ("xT", flip(x)), ("adj", np.ascontiguousarray(adj)), ("adjT", flip(adj)),
        ("wqT", flip(inputs["L0_gnn_Wq"])), ("wkT", flip(inputs["L0_gnn_Wk"])),
        ("wvT", flip(inputs["L0_gnn_Wv"])), ("woT", flip(inputs["L0_gnn_Wo"])),
        ("router_w", np.ascontiguousarray(inputs["L1_gnn_router_w"])),
        ("router_b", np.ascontiguousarray(inputs["L1_gnn_router_b"]).reshape(1, -1)),
        ("experts", np.ascontiguousarray(inputs["L1_gnn_expert_w"])),
        ("gammaT", flip(inputs["L1_gnn_bn_gamma"])), ("betaT", flip(inputs["L1_gnn_bn_beta"])),
    ]
    nc = bacc.Bacc("TRN2", target_bir_lowering=False, num_devices=1, dynamic_dma_scratch_size=1024)
    arrays, args = {}, []
    for name, a in laid:
        arrays[f"in_{name}"] = a
        args.append(nc.dram_tensor(f"in_{name}", a.shape, mybir.dt.from_np(a.dtype), kind="ExternalInput").ap())
    args.append(nc.dram_tensor("out_0", _OUT, F32, kind="ExternalOutput").ap())
    build_gnn_layers(nc, *args)
    r = run_bass_kernel_spmd(nc, [arrays], core_ids=[0])
    return r.results[0]["out_0"]
```
